# Optimizing a Trainium2 kernel written in Bass

```python
import numpy as np
import jax
import jax.numpy as jnp

def _softmax(x, axis=-1):
    return jax.nn.softmax(x, axis=axis)

def _gelu(x):
    return jax.nn.gelu(x, approximate=True)

def _silu(x):
    return jax.nn.silu(x)

def _sigmoid(x):
    return jax.nn.sigmoid(x)

def _layernorm(x, axis=-1, eps=1e-05):
    m = jnp.mean(x, axis=axis, keepdims=True)
    v = jnp.var(x, axis=axis, keepdims=True)
    return (x - m) / jnp.sqrt(v + eps)

def _scatter_add(tgt, idx, src, axis=0):
    return tgt.at[idx].add(src)

def _segment_sum(src, seg, n):
    return jax.ops.segment_sum(src, seg, n)
kernel_name = 'mk_prb_d2_jaxref_r4_c83c49'

def setup_inputs(seed: int=0):
    np.random.seed(seed)
    _w = jnp.asarray

    def _L0_attn_setup():
        import jax, jax.numpy as jnp
        import numpy as np
        DIM = 256
        MULT = 1
        HID = DIM * MULT
        C = 8.0
        key = jax.random.key(seed)
        k_x, k_wa, k_wx, k_lam = jax.random.split(key, 4)
        B, T = (8, 1024)
        x = jax.random.normal(k_x, (B, T, DIM), dtype=jnp.float32)
        std = DIM ** (-0.5)
        Wa = jax.random.normal(k_wa, (HID, DIM), dtype=jnp.float32) * std
        Wx = jax.random.normal(k_wx, (HID, DIM), dtype=jnp.float32) * std
        ba = jnp.zeros((HID,), dtype=jnp.float32)
        bx = jnp.zeros((HID,), dtype=jnp.float32)
        lo = float(np.log(0.9 / 0.1))
        hi = float(np.log(0.999 / 0.001))
        Lam = jax.random.uniform(k_lam, (HID,), dtype=jnp.float32, minval=lo, maxval=hi)
        return {'x': x, 'Wa': Wa, 'Wx': Wx, 'ba': ba, 'bx': bx, 'Lam': Lam}
    _L0_attn_in = _L0_attn_setup()

    def _L0_ffn_setup():
        import jax, jax.numpy as jnp
        import numpy as np
        N_HEAD, N_ACTIVE, D_MODEL, D_ATTN = (16, 4, 256, 64)
        key = jax.random.key(seed)
        ks = jax.random.split(key, 12)
        s = 0.02
        B, S = (2, 1024)
        return {'x': jax.random.normal(ks[0], (B, S, D_MODEL), dtype=jnp.float32), 'Wq': jax.random.normal(ks[1], (D_MODEL, N_HEAD * D_ATTN), dtype=jnp.float32) * s, 'bq': jnp.zeros((N_HEAD * D_ATTN,), dtype=jnp.float32), 'Wk': jax.random.normal(ks[2], (D_MODEL, N_HEAD * D_ATTN), dtype=jnp.float32) * s, 'bk': jnp.zeros((N_HEAD * D_ATTN,), dtype=jnp.float32), 'Wv': jax.random.normal(ks[3], (D_MODEL, N_HEAD * D_ATTN), dtype=jnp.float32) * s, 'bv': jnp.zeros((N_HEAD * D_ATTN,), dtype=jnp.float32), 'Wr': jax.random.normal(ks[4], (D_MODEL, N_HEAD), dtype=jnp.float32) * s, 'br': jnp.zeros((N_HEAD,), dtype=jnp.float32), 'Wo': jax.random.normal(ks[5], (N_ACTIVE * D_ATTN, D_MODEL), dtype=jnp.float32) * s, 'bo': jnp.zeros((D_MODEL,), dtype=jnp.float32)}
    _L0_ffn_in = _L0_ffn_setup()

    def _L1_attn_setup():
        import jax, jax.numpy as jnp
        import numpy as np
        D_MODEL = 256
        NUM_HEADS = 16
        D_HEAD = D_MODEL // NUM_HEADS
        NEG_BIG = 10000000000.0
        key = jax.random.key(seed)
        ks = jax.random.split(key, 9)
        d = D_MODEL
        scale = 1.0 / np.sqrt(d)
        inp = {'x': jax.random.normal(ks[0], (2, 512, d), dtype=jnp.float32), 'W_q': jax.random.normal(ks[1], (d, d), dtype=jnp.float32) * scale, 'b_q': jnp.zeros((d,), dtype=jnp.float32), 'W_k': jax.random.normal(ks[2], (d, d), dtype=jnp.float32) * scale, 'b_k': jnp.zeros((d,), dtype=jnp.float32), 'W_v': jax.random.normal(ks[3], (d, d), dtype=jnp.float32) * scale, 'b_v': jnp.zeros((d,), dtype=jnp.float32), 'W_o': jax.random.normal(ks[4], (d, d), dtype=jnp.float32) * scale, 'b_o': jnp.zeros((d,), dtype=jnp.float32)}
        return inp
    _L1_attn_in = _L1_attn_setup()

    def _L1_ffn_setup():
        import jax, jax.numpy as jnp
        import numpy as np
        DIM = 256

        def _reference_tuple_inner(x, W_r, W_k, W_v, mu_r, mu_k):
            B, T, C = x.shape
            x_prev = jnp.concatenate([jnp.zeros((B, 1, C), x.dtype), x[:, :-1, :]], axis=1)
            xr = mu_r * x + (1.0 - mu_r) * x_prev
            xk = mu_k * x + (1.0 - mu_k) * x_prev
            r = jax.nn.sigmoid(jnp.einsum('btc,dc->btd', xr, W_r))
            k = jnp.einsum('btc,dc->btd', xk, W_k)
            k_act = jnp.square(jax.nn.relu(k))
            out = r * jnp.einsum('btc,dc->btd', k_act, W_v)
            new_state = x[:, -1, :]
            return (out, new_state)
        key = jax.random.key(seed)
        ks = jax.random.split(key, 6)
        B, T, C = (8, 512, DIM)
        x = jax.random.normal(ks[0], (B, T, C), dtype=jnp.float32)
        s = 1.0 / np.sqrt(C)
        W_r = jax.random.uniform(ks[1], (C, C), jnp.float32, -s, s)
        W_k = jax.random.uniform(ks[2], (C, C), jnp.float32, -s, s)
        W_v = jax.random.uniform(ks[3], (C, C), jnp.float32, -s, s)
        mu_r = jax.random.uniform(ks[4], (C,), jnp.float32)
        mu_k = jax.random.uniform(ks[5], (C,), jnp.float32)
        return {'x': x, 'W_r': W_r, 'W_k': W_k, 'W_v': W_v, 'mu_r': mu_r, 'mu_k': mu_k}
    _L1_ffn_in = _L1_ffn_setup()
    _d = {'L0_attn_x': _L0_attn_in['x'], 'L0_attn_Wa': _L0_attn_in['Wa'], 'L0_attn_Wx': _L0_attn_in['Wx'], 'L0_attn_ba': _L0_attn_in['ba'], 'L0_attn_bx': _L0_attn_in['bx'], 'L0_attn_Lam': _L0_attn_in['Lam'], 'L0_ffn_Wq': _L0_ffn_in['Wq'], 'L0_ffn_bq': _L0_ffn_in['bq'], 'L0_ffn_Wk': _L0_ffn_in['Wk'], 'L0_ffn_bk': _L0_ffn_in['bk'], 'L0_ffn_Wv': _L0_ffn_in['Wv'], 'L0_ffn_bv': _L0_ffn_in['bv'], 'L0_ffn_Wr': _L0_ffn_in['Wr'], 'L0_ffn_br': _L0_ffn_in['br'], 'L0_ffn_Wo': _L0_ffn_in['Wo'], 'L0_ffn_bo': _L0_ffn_in['bo'], 'L1_attn_W_q': _L1_attn_in['W_q'], 'L1_attn_b_q': _L1_attn_in['b_q'], 'L1_attn_W_k': _L1_attn_in['W_k'], 'L1_attn_b_k': _L1_attn_in['b_k'], 'L1_attn_W_v': _L1_attn_in['W_v'], 'L1_attn_b_v': _L1_attn_in['b_v'], 'L1_attn_W_o': _L1_attn_in['W_o'], 'L1_attn_b_o': _L1_attn_in['b_o'], 'L1_ffn_W_r': _L1_ffn_in['W_r'], 'L1_ffn_W_k': _L1_ffn_in['W_k'], 'L1_ffn_W_v': _L1_ffn_in['W_v'], 'L1_ffn_mu_r': _L1_ffn_in['mu_r'], 'L1_ffn_mu_k': _L1_ffn_in['mu_k']}
    _x0 = _d['L0_attn_x']
    _d['L0_attn_x'] = jax.random.normal(jax.random.fold_in(jax.random.key(seed), 1), (4, 2048, 256), dtype=_x0.dtype)
    del _x0
    return _d

def reference(L0_attn_x, L0_attn_Wa, L0_attn_Wx, L0_attn_ba, L0_attn_bx, L0_attn_Lam, L0_ffn_Wq, L0_ffn_bq, L0_ffn_Wk, L0_ffn_bk, L0_ffn_Wv, L0_ffn_bv, L0_ffn_Wr, L0_ffn_br, L0_ffn_Wo, L0_ffn_bo, L1_attn_W_q, L1_attn_b_q, L1_attn_W_k, L1_attn_b_k, L1_attn_W_v, L1_attn_b_v, L1_attn_W_o, L1_attn_b_o, L1_ffn_W_r, L1_ffn_W_k, L1_ffn_W_v, L1_ffn_mu_r, L1_ffn_mu_k):

    def _L0_attn_ref(x, Wa, Wx, ba, bx, Lam):
        import jax, jax.numpy as jnp
        import numpy as np
        DIM = 256
        MULT = 1
        HID = DIM * MULT
        C = 8.0
        r = jax.nn.sigmoid(jnp.einsum('btd,dh->bth', x, Wa) + ba)
        i = jax.nn.sigmoid(jnp.einsum('btd,dh->bth', x, Wx) + bx)
        a = jax.nn.sigmoid(Lam)
        at = a * jnp.exp(-r * jnp.log(jnp.asarray(C, x.dtype)))
        bt = jnp.sqrt(1.0 - at * at) * (i * x)

        def combine(e1, e2):
            a1, b1 = e1
            a2, b2 = e2
            return (a2 * a1, a2 * b1 + b2)
        _, y = jax.lax.associative_scan(combine, (at, bt), axis=1)
        return y

    def _L0_ffn_ref(x, Wq, bq, Wk, bk, Wv, bv, Wr, br, Wo, bo):
        import jax, jax.numpy as jnp
        import numpy as np
        N_HEAD, N_ACTIVE, D_MODEL, D_ATTN = (16, 4, 256, 64)
        B, S, D = x.shape
        H, K, dh = (N_HEAD, N_ACTIVE, D_ATTN)
        dist = jax.nn.softmax(jnp.mean(x @ Wr + br, axis=1), axis=-1)
        top_vals, top_idx = jax.lax.top_k(dist, K)
        sparse = jnp.zeros_like(dist).at[jnp.arange(B)[:, None], top_idx].set(top_vals)
        gates_all = jax.nn.softmax(sparse, axis=1)
        g = jnp.take_along_axis(gates_all, top_idx, axis=1)[:, :, None, None]

        def proj(W, b):
            return (x @ W + b).reshape(B, S, H, dh).transpose(0, 2, 1, 3)
        Q, Kt, V = (proj(Wq, bq), proj(Wk, bk), proj(Wv, bv))
        idx = top_idx[:, :, None, None]
        Qk = jnp.take_along_axis(Q, idx, axis=1) * g
        Kk = jnp.take_along_axis(Kt, idx, axis=1) * g
        Vk = jnp.take_along_axis(V, idx, axis=1) * g
        scores = jnp.einsum('bksd,bktd->bkst', Qk, Kk) / jnp.sqrt(jnp.float32(dh))
        attn = jax.nn.softmax(scores, axis=-1)
        out = jnp.einsum('bkst,bktd->bksd', attn, Vk)
        out = out.transpose(0, 2, 1, 3).reshape(B, S, K * dh)
        return out @ Wo + bo

    def _L1_attn_ref(x, W_q, b_q, W_k, b_k, W_v, b_v, W_o, b_o):
        import jax, jax.numpy as jnp
        import numpy as np
        D_MODEL = 256
        NUM_HEADS = 16
        D_HEAD = D_MODEL // NUM_HEADS
        NEG_BIG = 10000000000.0
        B, S, d = x.shape
        H, Dh = (NUM_HEADS, D_HEAD)
        Q = x @ W_q + b_q
        K = x @ W_k + b_k
        V = x @ W_v + b_v
        Qh = Q.reshape(B, S, H, Dh).transpose(0, 2, 1, 3)
        Kh = K.reshape(B, S, H, Dh).transpose(0, 2, 1, 3)
        Vh = V.reshape(B, S, H, Dh).transpose(0, 2, 1, 3)
        scores = jnp.einsum('bhid,bhjd->bhij', Qh, Kh) / jnp.sqrt(jnp.asarray(Dh, dtype=x.dtype))
        causal = jnp.tril(jnp.ones((S, S), dtype=x.dtype))
        scores = scores * causal - NEG_BIG * (1.0 - causal)
        attn = jax.nn.softmax(scores, axis=-1)
        vals = jnp.einsum('bhij,bhjd->bhid', attn, Vh)
        vals = vals.transpose(0, 2, 1, 3).reshape(B, S, d)
        return vals @ W_o + b_o

    def _L1_ffn_ref(x, W_r, W_k, W_v, mu_r, mu_k):
        import jax, jax.numpy as jnp
        import numpy as np
        DIM = 256

        def _reference_tuple_inner(x, W_r, W_k, W_v, mu_r, mu_k):
            B, T, C = x.shape
            x_prev = jnp.concatenate([jnp.zeros((B, 1, C), x.dtype), x[:, :-1, :]], axis=1)
            xr = mu_r * x + (1.0 - mu_r) * x_prev
            xk = mu_k * x + (1.0 - mu_k) * x_prev
            r = jax.nn.sigmoid(jnp.einsum('btc,dc->btd', xr, W_r))
            k = jnp.einsum('btc,dc->btd', xk, W_k)
            k_act = jnp.square(jax.nn.relu(k))
            out = r * jnp.einsum('btc,dc->btd', k_act, W_v)
            new_state = x[:, -1, :]
            return (out, new_state)
        return _reference_tuple_inner(x, W_r, W_k, W_v, mu_r, mu_k)[0]
    x = L0_attn_x
    xn = _layernorm(x, axis=-1)
    x = x + _L0_attn_ref(xn, L0_attn_Wa, L0_attn_Wx, L0_attn_ba, L0_attn_bx, L0_attn_Lam) + _L0_ffn_ref(xn, L0_ffn_Wq, L0_ffn_bq, L0_ffn_Wk, L0_ffn_bk, L0_ffn_Wv, L0_ffn_bv, L0_ffn_Wr, L0_ffn_br, L0_ffn_Wo, L0_ffn_bo)
    xn = _layernorm(x, axis=-1)
    x = x + _L1_attn_ref(xn, L1_attn_W_q, L1_attn_b_q, L1_attn_W_k, L1_attn_b_k, L1_attn_W_v, L1_attn_b_v, L1_attn_W_o, L1_attn_b_o) + _L1_ffn_ref(xn, L1_ffn_W_r, L1_ffn_W_k, L1_ffn_W_v, L1_ffn_mu_r, L1_ffn_mu_k)
    return x

_drawn_inputs = setup_inputs


def setup_inputs(seed=0):
    import zlib

    import numpy as np

    out = dict(_drawn_inputs(seed))
    spreads = {'L0_attn_ba': (0.0, 0.8),
     'L0_attn_bx': (0.0, 0.573),
     'L0_ffn_bq': (0.0, 2.0),
     'L0_ffn_bk': (0.0, 2.0),
     'L0_ffn_bv': (0.0, 0.8),
     'L0_ffn_br': (0.0, 0.8),
     'L0_ffn_bo': (0.0, 0.1),
     'L1_attn_b_q': (0.0, 0.8),
     'L1_attn_b_k': (0.0, 2.0),
     'L1_attn_b_v': (0.0, 0.1),
     'L1_attn_b_o': (0.0, 0.1)}
    factors = {'L0_attn_Lam': 8.0,
     'L0_ffn_Wq': 64.0,
     'L0_ffn_Wk': 64.0,
     'L0_ffn_Wv': 57.193,
     'L0_ffn_Wr': 8.0,
     'L0_ffn_Wo': 8.0,
     'L1_ffn_W_r': 4.384,
     'L1_ffn_mu_r': 8.0}
    for name, (base, spread) in spreads.items():
        noise = np.random.default_rng([zlib.crc32(name.encode()), seed]).standard_normal(out[name].shape)
        drawn = base * np.exp(spread * noise) if base else spread * noise
        out[name] = jnp.asarray(drawn.astype(out[name].dtype))
    for name, factor in factors.items():
        out[name] = (out[name] * factor).astype(out[name].dtype)
    return out
```

```python
from contextlib import ExitStack

import numpy as np

import concourse.bass as bass
from concourse import mybir

ALU = mybir.AluOpType
ACT = mybir.ActivationFunctionType
AX = mybir.AxisListType
F32 = mybir.dt.float32
F32R = mybir.dt.float32r
BF16 = mybir.dt.bfloat16
U32 = mybir.dt.uint32

P = 128
B, T, D = 4, 2048, 256
C = D // P
BLOCK = 512
S = BLOCK // P
QB = T // BLOCK
NBLK = B * QB
KT = T // P
H0, K0, DH0 = 16, 4, 64
H1, DH1 = 16, 16
G1 = 4
EPS = 1e-5
LN8 = float(np.log(np.float32(8.0)))
LOWEST = -3.0e38


class Step:

    def __init__(self, i, k, unroll):
        self.t = i * unroll + k
        self.slot = k % 2
        self.turn = i * (unroll // 2) + k // 2
        self.q = k % QB
        self.b = i * (unroll // QB) + k // QB
        self.side = k // QB % 2
        self.uses = i * (unroll // (2 * QB)) + k // (2 * QB)


def pipelined(e, n, unroll, body, ahead=1, behind=1):
    last = n // unroll - 1

    def edge(current):
        def at(d):
            t = current + d
            return Step(t // unroll, t % unroll, unroll) if 0 <= t < n else None
        body(at)

    for t in range(-ahead, unroll + behind):
        edge(t)
    with e.Fori(1, last) as i:
        for k in range(behind, unroll + behind):
            body(lambda d: Step(i, k + d, unroll))
    for t in range(last * unroll + behind, n + behind):
        edge(t)


def wait(e, sem, value):
    if isinstance(value, int) and value <= 0:
        return
    e.wait_ge(sem, value)


def hold(e, passed):
    e.sem_inc(passed, 1)


def names(nc, ctx, phase):
    def sb(name, shape, dt=F32):
        return ctx.enter_context(nc.sbuf_tensor(f"{phase}_{name}", shape, dt))

    def pb(name, shape, dt=F32):
        return ctx.enter_context(nc.psum_tensor(f"{phase}_{name}", shape, dt))

    def sem(name, n=None):
        if n is None:
            return ctx.enter_context(nc.semaphore(f"{phase}_{name}"))
        return [ctx.enter_context(nc.semaphore(f"{phase}_{name}{i}")) for i in range(n)]

    return sb, pb, sem


def at_step(view, index):
    return view[bass.ds(index, 1)].squeeze(0) if not isinstance(index, int) else view[index]


def constants(nc, ident, fold, upper):
    with ExitStack() as ctx:
        _, _, sem = names(nc, ctx, "constants")
        cleared, shaped = sem("cleared"), sem("shaped")
        block = ctx.enter_context(nc.Block())

        @block.gpsimd
        def _(e):
            e.memset(ident, 0.0).then_inc(cleared, 1)
            e.memset(fold, 0.0).then_inc(cleared, 1)
            e.memset(upper, 0.0).then_inc(cleared, 1)
            e.wait_ge(cleared, 3)
            e.affine_select(out=ident, in_=ident, compare_op=ALU.not_equal, fill=1.0, base=0,
                            pattern=[[-1, P]], channel_multiplier=1).then_inc(shaped, 1)
            e.affine_select(out=fold, in_=fold, compare_op=ALU.not_equal, fill=1.0, base=0,
                            pattern=[[-1, DH0]], channel_multiplier=1).then_inc(shaped, 1)
            e.affine_select(out=upper[:, BLOCK - P:], in_=upper[:, BLOCK - P:], compare_op=ALU.is_ge, fill=LOWEST, base=0,
                            pattern=[[-1, P]], channel_multiplier=1).then_inc(shaped, 1)
            e.wait_ge(shaped, 3)
            e.affine_select(out=fold, in_=fold, compare_op=ALU.not_equal, fill=1.0, base=-DH0,
                            pattern=[[-1, DH0]], channel_multiplier=1).then_inc(shaped, 1)
            e.wait_ge(shaped, 4)


def recurrence(nc, x, Wa, Wx, ba, bx, Lam, xnT, yT, means, ident):
    x_v = x.rearrange("b (q s p) d -> (b q) p s d", p=P, s=S)
    xnT_v = xnT.rearrange("(c p) (t n) -> t p c n", p=P, n=BLOCK)
    yT_v = yT.rearrange("(c p) (t n) -> t p c n", p=P, n=BLOCK)
    with ExitStack() as ctx:
        sb, pb, sem = names(nc, ctx, "recurrence")
        wa, wx = sb("wa", [P, C, D]), sb("wx", [P, C, D])
        bias_r, bias_i = sb("bias_r", [P, C]), sb("bias_i", [P, C])
        lam, decay = sb("lam", [P, C]), sb("decay", [P, C])
        eps, quarter, ones = sb("eps", [P, 1]), sb("quarter", [P, 1]), sb("ones", [P, 1])
        xin, xn = sb("xin", [P, 2, S, D]), sb("xn", [P, 2, S, D])
        st, mv = sb("st", [P, S, 6]), sb("mv", [P, S, 2])
        dev, inv = sb("dev", [P, S]), sb("inv", [P, S])
        xt = sb("xt", [P, 2, C, BLOCK])
        tanh_r, tanh_i = sb("tanh_r", [P, C, BLOCK]), sb("tanh_i", [P, 2, C, BLOCK])
        at_raw, at = sb("at_raw", [P, C, BLOCK]), sb("at", [P, 2, C, BLOCK])
        at_sq, root = sb("at_sq", [P, C, BLOCK]), sb("root", [P, 2, C, BLOCK])
        drive = sb("drive", [P, C, BLOCK])
        y = sb("y", [P, 2, C, BLOCK])
        turn_ps = pb("turn_ps", [P, C, BLOCK])
        gate_ps = pb("gate_ps", [P, 2, C, BLOCK])
        mean_ps = [pb(f"mean_ps{c}", [P, BLOCK]) for c in range(C)]

        weights_in = sem("weights_in")
        consts, prepared = sem("consts"), sem("prepared")
        passed, pool_passed = sem("passed"), sem("pool_passed")
        x_in = sem("x_in", 2)
        stats, deviation, inverse, normed = sem("stats"), sem("deviation"), sem("inverse"), sem("normed")
        turned, xt_ready = sem("turned"), sem("xt_ready")
        gates_ready, squashed, decayed = sem("gates_ready"), sem("squashed"), sem("decayed")
        clamped, squared, rooted = sem("clamped"), sem("squared"), sem("rooted")
        driven, scanned, summed = sem("driven"), sem("scanned"), sem("summed")
        xt_out, y_out = sem("xt_out", 2), sem("y_out", 2)
        block = ctx.enter_context(nc.Block())

        @block.sync
        def _(e):
            def load(s):
                wait(e, normed, (s.t - 1) * S)
                e.dma_start(xin[:, s.slot], at_step(x_v, s.t)).then_inc(x_in[s.slot], 16)

            def body(at_):
                nxt, cur = at_(2), at_(0)
                if nxt is not None:
                    load(nxt)
                if cur is not None:
                    e.wait_ge(xt_ready, (cur.t + 1) * C)
                    e.dma_start(at_step(xnT_v, cur.t), xt[:, cur.slot]).then_inc(xt_out[cur.slot], 16)
                    e.wait_ge(scanned, (cur.t + 1) * C)
                    e.dma_start(at_step(yT_v, cur.t), y[:, cur.slot]).then_inc(y_out[cur.slot], 16)

            for w, v in ((wa, Wa), (wx, Wx)):
                e.dma_start(w[:], v.rearrange("(c p) h -> p c h", p=P)).then_inc(weights_in, 16)
            for w, v in ((bias_r, ba), (bias_i, bx), (lam, Lam)):
                e.dma_start(w[:], v.rearrange("(c p) -> p c", p=P), allow_slow_non_contiguous=True).then_inc(weights_in, 16)
            pipelined(e, NBLK, 4, body, ahead=2)
            for slot in range(2):
                e.wait_ge(xt_out[slot], 16 * NBLK // 2)
                e.wait_ge(y_out[slot], 16 * NBLK // 2)

        @block.vector
        def _(e):
            e.memset(eps[:], EPS).then_inc(consts, 1)
            e.memset(quarter[:], 0.25).then_inc(consts, 1)
            e.memset(ones[:], 1.0).then_inc(consts, 1)
            e.wait_ge(weights_in, 16 * 5)
            e.tensor_scalar(bias_r[:], bias_r[:], 0.5, None, ALU.mult).then_inc(prepared, 1)
            e.tensor_scalar(bias_i[:], bias_i[:], 0.5, None, ALU.mult).then_inc(prepared, 1)
            e.wait_ge(prepared, 3)
            e.tensor_scalar(decay[:], decay[:], 1.0, None, ALU.add).then_inc(prepared, 1)
            e.wait_ge(prepared, 4)
            e.reciprocal(lam[:], decay[:]).then_inc(prepared, 1)
            e.wait_ge(prepared, 6)
            e.tensor_scalar(decay[:], decay[:], -0.5 * LN8, None, ALU.add).then_inc(prepared, 1)

            def body(at_):
                nxt, cur = at_(1), at_(0)
                if nxt is not None:
                    s = nxt
                    e.wait_ge(x_in[s.slot], (s.turn + 1) * 16)
                    for j in range(S):
                        e.bn_stats(st[:, j], xin[:, s.slot, j]).then_inc(stats, 1)
                    e.wait_ge(stats, s.t * 2 * S + S)
                    hold(e, passed)
                    for j in range(S):
                        e.bn_aggr(mv[:, j], st[:, j]).then_inc(stats, 1)
                    e.wait_ge(deviation, s.t + 1)
                    e.reciprocal(inv[:], dev[:]).then_inc(inverse, 1)
                    wait(e, turned, s.t - 1)
                    e.wait_ge(inverse, s.t + 1)
                    for j in range(S):
                        e.tensor_scalar(xn[:, s.slot, j], xin[:, s.slot, j], mv[:, j, 0:1], inv[:, j:j + 1],
                                        ALU.subtract, ALU.mult).then_inc(normed, 1)
                if cur is not None:
                    s = cur
                    e.wait_ge(squashed, (s.t + 1) * 2 * C)
                    e.wait_ge(xt_ready, (s.t + 1) * C)
                    wait(e, scanned, s.t * C)
                    e.scalar_tensor_tensor(out=drive[:], in0=tanh_i[:, s.slot], scalar=1.0, in1=xt[:, s.slot],
                                           op0=ALU.add, op1=ALU.mult).then_inc(driven, 1)
                    e.wait_ge(driven, s.t * 2 + 1)
                    e.wait_ge(rooted, s.t + 1)
                    e.tensor_tensor(drive[:], drive[:], root[:, s.slot], ALU.mult).then_inc(driven, 1)
                    e.wait_ge(driven, s.t * 2 + 2)
                    e.wait_ge(clamped, s.t + 1)
                    wait(e, y_out[s.slot], s.turn * 16)
                    for c in range(C):
                        start = 0.0 if s.q == 0 else y[:, 1 - s.slot, c, BLOCK - 1:BLOCK]
                        e.tensor_tensor_scan(y[:, s.slot, c], at[:, s.slot, c], drive[:, c], start,
                                             ALU.mult, ALU.add).then_inc(scanned, 1)

            def sums(s):
                if s is not None and s.q == QB - 1:
                    e.wait_ge(turned, s.t + 1)
                    for c in range(C):
                        e.tensor_copy(means[:, c, bass.ds(s.b, 1)], mean_ps[c][:, 0:1]).then_inc(summed, 1)

            def both(at_):
                body(at_)
                sums(at_(1))

            pipelined(e, NBLK, 4, both)

        @block.scalar
        def _(e):
            e.wait_ge(weights_in, 16 * 5)
            e.wait_ge(prepared, 2)
            e.activation(decay[:], lam[:], ACT.Exp, scale=-1.0).then_inc(prepared, 1)
            e.wait_ge(prepared, 5)
            e.activation(decay[:], lam[:], ACT.Ln).then_inc(prepared, 1)
            e.wait_ge(prepared, 7)
            e.wait_ge(consts, 3)

            def body(at_):
                nxt, cur = at_(1), at_(0)
                if nxt is not None:
                    e.wait_ge(stats, (nxt.t + 1) * 2 * S)
                    e.activation(dev[:], mv[:, :, 1], ACT.Sqrt, bias=eps[:, 0:1]).then_inc(deviation, 1)
                if cur is not None:
                    s = cur
                    for c in range(C):
                        e.wait_ge(gates_ready, s.t * 2 * C + c + 1)
                        e.activation(tanh_r[:, c], gate_ps[:, 0, c], ACT.Tanh, bias=bias_r[:, c:c + 1],
                                     scale=0.5).then_inc(squashed, 1)
                    wait(e, driven, (s.t - 1) * 2)
                    for c in range(C):
                        e.wait_ge(gates_ready, s.t * 2 * C + C + c + 1)
                        e.activation(tanh_i[:, s.slot, c], gate_ps[:, 1, c], ACT.Tanh, bias=bias_i[:, c:c + 1],
                                     scale=0.5).then_inc(squashed, 1)
                    for c in range(C):
                        e.wait_ge(squashed, s.t * 2 * C + c + 1)
                        e.activation(at_raw[:, c], tanh_r[:, c], ACT.Exp, bias=decay[:, c:c + 1],
                                     scale=-0.5 * LN8).then_inc(decayed, 1)
                    e.wait_ge(squared, s.t + 1)
                    e.activation(root[:, s.slot], at_sq[:], ACT.Sqrt, bias=quarter[:, 0:1],
                                 scale=-0.25).then_inc(rooted, 1)
                if nxt is not None:
                    s = nxt
                    e.wait_ge(turned, s.t + 1)
                    wait(e, driven, (s.t - 1) * 2)
                    wait(e, xt_out[s.slot], s.turn * 16)
                    for c in range(C):
                        e.activation(xt[:, s.slot, c], turn_ps[:, c], ACT.Copy).then_inc(xt_ready, 1)

            pipelined(e, NBLK, 4, body)

        @block.gpsimd
        def _(e):
            def body(at_):
                nxt, cur = at_(1), at_(0)
                if cur is None:
                    return
                s = cur
                wait(e, scanned, (s.t - 1) * C)
                e.wait_ge(decayed, (s.t + 1) * C)
                hold(e, pool_passed)
                e.tensor_scalar(at[:, s.slot], at_raw[:], 1.0, 0.0, ALU.min, ALU.max).then_inc(clamped, 1)
                e.wait_ge(clamped, s.t + 1)
                e.tensor_tensor(at_sq[:], at[:, s.slot], at[:, s.slot], ALU.mult).then_inc(squared, 1)

            pipelined(e, NBLK, 4, body)

        @block.tensor
        def _(e):
            e.wait_ge(weights_in, 16 * 5)
            e.wait_ge(consts, 3)

            def body(at_):
                nxt, cur = at_(1), at_(0)
                if cur is not None:
                    s = cur
                    e.wait_ge(xt_ready, (s.t + 1) * C)
                    wait(e, squashed, s.t * 2 * C)
                    for g, w in enumerate((wa, wx)):
                        for o in range(C):
                            for c in range(C):
                                mm = e.matmul(gate_ps[:, g, o], w[:, c, o * P:(o + 1) * P], xt[:, s.slot, c],
                                              start=(c == 0), stop=(c == C - 1))
                            mm.then_inc(gates_ready, 1)
                if nxt is not None:
                    s = nxt
                    e.wait_ge(normed, (s.t + 1) * S)
                    wait(e, xt_ready, s.t * C)
                    if s.q == 0:
                        wait(e, summed, s.b * C)
                    for j in range(S):
                        for c in range(C):
                            tile = xn[:, s.slot, j, c * P:(c + 1) * P]
                            e.transpose(turn_ps[:, c, j * P:(j + 1) * P], tile, ident)
                            mm = e.matmul(mean_ps[c][:, 0:1], tile, ones[:], start=(s.q == 0 and j == 0),
                                          stop=(s.q == QB - 1 and j == S - 1))
                    mm.then_inc(turned, 1)

            pipelined(e, NBLK, 4, body)


def route(nc, means, Wr, br, chosen, gates):
    with ExitStack() as ctx:
        sb, pb, sem = names(nc, ctx, "route")
        wr, brow = sb("wr", [P, C, H0]), sb("brow", [B, H0])
        logits, weights = sb("logits", [B, H0]), sb("weights", [B, H0])
        top, neg, total = sb("top", [B, 8]), sb("neg", [B, 1]), sb("total", [B, 1])
        best, place = sb("best", [B, 8]), sb("place", [B, 8], U32)
        ex, rest, norm, gate = sb("ex", [B, K0]), sb("rest", [B, 1]), sb("norm", [B, 1]), sb("gate", [B, K0])
        lin = pb("lin", [B, BLOCK])
        loaded, projected, step, exp_done, stored = (sem("loaded"), sem("projected"), sem("step"),
                                                     sem("exp_done"), sem("stored"))
        block = ctx.enter_context(nc.Block())

        @block.sync
        def _(e):
            e.dma_start(wr[:], Wr.rearrange("(c p) h -> p c h", p=P)).then_inc(loaded, 16)
            e.dma_start(brow[:], br.partition_broadcast(B)).then_inc(loaded, 16)
            e.wait_ge(step, 12)
            e.dma_start(chosen.rearrange("(b k) -> b k", k=K0), place[:, 0:K0]).then_inc(stored, 16)
            e.dma_start(gates.rearrange("(b k) -> b k", k=K0), gate[:]).then_inc(stored, 16)
            e.wait_ge(stored, 32)

        @block.tensor
        def _(e):
            e.wait_ge(loaded, 32)
            for c in range(C):
                mm = e.matmul(lin[:, 0:H0], means[:, c, :], wr[:, c, :], start=(c == 0), stop=(c == C - 1))
            mm.then_inc(projected, 1)

        @block.scalar
        def _(e):
            e.wait_ge(step, 3)
            e.activation(weights[:], logits[:], ACT.Exp, bias=neg[:, 0:1], accum_out=total[:]).then_inc(exp_done, 1)
            e.wait_ge(step, 8)
            e.activation(ex[:], best[:, 0:K0], ACT.Exp, bias=neg[:, 0:1], accum_out=norm[:]).then_inc(exp_done, 1)
            e.activation(rest[:], neg[:], ACT.Exp).then_inc(exp_done, 1)

        @block.vector
        def _(e):
            count = [0]

            def link(ins):
                count[0] += 1
                ins.then_inc(step, 1)
                e.wait_ge(step, count[0])

            e.wait_ge(projected, 1)
            link(e.scalar_tensor_tensor(out=logits[:], in0=lin[:, 0:H0], scalar=1.0 / T, in1=brow[:],
                                        op0=ALU.mult, op1=ALU.add))
            link(e.max(top[:], logits[:]))
            link(e.tensor_scalar(neg[:], top[:, 0:1], -1.0, None, ALU.mult))
            e.wait_ge(exp_done, 1)
            link(e.reciprocal(total[:], total[:]))
            link(e.tensor_scalar(weights[:], weights[:], total[:, 0:1], None, ALU.mult))
            link(e.max(best[:], weights[:]))
            link(e.max_index(place[:], best[:], weights[:]))
            link(e.tensor_scalar(neg[:], best[:, 0:1], -1.0, None, ALU.mult))
            e.wait_ge(exp_done, 3)
            link(e.tensor_scalar(rest[:], rest[:], float(H0 - K0), None, ALU.mult))
            link(e.tensor_tensor(norm[:], norm[:], rest[:], ALU.add))
            link(e.reciprocal(norm[:], norm[:]))
            link(e.tensor_scalar(gate[:], ex[:], norm[:, 0:1], None, ALU.mult))


def project0(nc, xnT, Wq, Wk, Wv, bq, bk, bv, chosen, qk_hi, qk_lo, v0):
    xnT_v = xnT.rearrange("(c p) (t n) -> t p c n", p=P, n=BLOCK)
    hi_v, lo_v = (a.rearrange("r (b o u) d (q n) -> b q r (u d) o n", b=B, o=2, n=BLOCK) for a in (qk_hi, qk_lo))
    v0_v = v0.rearrange("(b k) p (q s) d -> b q k p s d", b=B, s=S)
    with ExitStack() as ctx:
        sb, pb, sem = names(nc, ctx, "project0")
        picks = sb("picks", [1, B * K0], U32)
        wq, wk, wv = (sb(f"w{n}", [P, C, K0 * DH0]) for n in "qkv")
        bias = sb("bias", [P, 4])
        bias_v = sb("bias_v", [P, K0 * DH0])
        xt = sb("xt", [P, 2, C, BLOCK])
        hi, lo = sb("hi", [P, 2, 4, BLOCK], F32R), sb("lo", [P, 2, 4, BLOCK], F32R)
        vs = sb("vs", [P, 2, S, K0 * DH0])
        qk_ps = pb("qk_ps", [P, 4, BLOCK])
        v_ps = pb("v_ps", [P, S, K0 * DH0])

        picks_in, weights_in, x_in = sem("picks_in"), sem("weights_in"), sem("x_in", 2)
        qk_ready, hi_ready, lo_ready = sem("qk_ready"), sem("hi_ready"), sem("lo_ready")
        v_ready, vs_ready, stored = sem("v_ready"), sem("vs_ready"), sem("stored", 2)
        STORES = 4 + K0
        LOADS = K0 * 6
        block = ctx.enter_context(nc.Block())

        @block.sync
        def _(e):
            e.dma_start(picks[:], chosen.rearrange("(o n) -> o n", o=1)).then_inc(picks_in, 16)
            e.wait_ge(picks_in, 16)

            def weights(s):
                wait(e, v_ready, s.t)
                wait(e, lo_ready, s.t * 4)
                wait(e, vs_ready, s.t)
                for k in range(K0):
                    h = e.value_load(picks[0:1, bass.ds(s.b * K0 + k, 1)], min_val=0, max_val=H0 - 1)
                    for w, v in ((wq, Wq), (wk, Wk), (wv, Wv)):
                        e.dma_start(w[:, :, k * DH0:(k + 1) * DH0], at_step(v.rearrange("(c p) (h d) -> h p c d", p=P, d=DH0), h))\
                            .then_inc(weights_in, 16)
                    half = slice(k % 2 * DH0, k % 2 * DH0 + DH0)
                    for o, v in ((0, bq), (2, bk)):
                        e.dma_start(bias[half, o + k // 2:o + k // 2 + 1], at_step(v.rearrange("(h d o) -> h d o", d=DH0, o=1), h))\
                            .then_inc(weights_in, 16)
                    e.dma_start(bias_v[:, k * DH0:(k + 1) * DH0],
                                at_step(bv.rearrange("(h d) -> h d", d=DH0), h).partition_broadcast(P)).then_inc(weights_in, 16)

            def body(at):
                nxt, cur = at(1), at(0)
                if nxt is not None:
                    wait(e, v_ready, nxt.t - 1)
                    e.dma_start(xt[:, nxt.slot], at_step(xnT_v, nxt.t)).then_inc(x_in[nxt.slot], 16)
                if cur is not None:
                    s = cur
                    if s.q == 0:
                        weights(s)
                    for ready, tile, view in ((hi_ready, hi, hi_v), (lo_ready, lo, lo_v)):
                        e.wait_ge(ready, (s.t + 1) * 4)
                        for r in range(2):
                            e.dma_start(at_step(view, s.b)[s.q, r], tile[:, s.slot, 2 * r:2 * r + 2].bitcast(F32)).then_inc(stored[s.slot], 16)
                    e.wait_ge(vs_ready, s.t + 1)
                    for k in range(K0):
                        e.dma_start(at_step(v0_v, s.b)[s.q, k], vs[:, s.slot, :, k * DH0:(k + 1) * DH0]).then_inc(stored[s.slot], 16)

            pipelined(e, NBLK, 4, body)
            for slot in range(2):
                e.wait_ge(stored[slot], 16 * STORES * NBLK // 2)

        @block.tensor
        def _(e):
            def body(at):
                s = at(0)
                if s is None:
                    return
                if s.q == 0:
                    e.wait_ge(weights_in, (s.b + 1) * 16 * LOADS)
                e.wait_ge(x_in[s.slot], (s.turn + 1) * 16)
                for o in range(4):
                    wait(e, lo_ready, (s.t - 1) * 4 + o + 1)
                    w = (wq, wk)[o // 2]
                    for c in range(C):
                        mm = e.matmul(qk_ps[:, o], w[:, c, o % 2 * P:(o % 2 + 1) * P], xt[:, s.slot, c],
                                      start=(c == 0), stop=(c == C - 1))
                    mm.then_inc(qk_ready, 1)
                wait(e, vs_ready, s.t)
                for j in range(S):
                    for c in range(C):
                        mm = e.matmul(v_ps[:, j], xt[:, s.slot, c, j * P:(j + 1) * P], wv[:, c],
                                      start=(c == 0), stop=(c == C - 1))
                mm.then_inc(v_ready, 1)

            pipelined(e, NBLK, 4, body)

        @block.scalar
        def _(e):
            def body(at):
                s = at(0)
                if s is None:
                    return
                wait(e, stored[s.slot], s.turn * 16 * STORES)
                for o in range(4):
                    e.wait_ge(qk_ready, s.t * 4 + o + 1)
                    e.activation(hi[:, s.slot, o], qk_ps[:, o], ACT.Identity, bias=bias[:, o:o + 1]).then_inc(hi_ready, 1)

            pipelined(e, NBLK, 4, body)

        @block.vector
        def _(e):
            def body(at):
                s = at(0)
                if s is None:
                    return
                wait(e, stored[s.slot], s.turn * 16 * STORES)
                for o in range(4):
                    e.wait_ge(hi_ready, s.t * 4 + o + 1)
                    e.scalar_tensor_tensor(out=lo[:, s.slot, o], in0=qk_ps[:, o], scalar=bias[:, o:o + 1],
                                           in1=hi[:, s.slot, o].bitcast(F32), op0=ALU.add, op1=ALU.subtract).then_inc(lo_ready, 1)
                e.wait_ge(v_ready, s.t + 1)
                e.tensor_tensor(vs[:, s.slot], v_ps[:], bias_v[:].unsqueeze(1).broadcast_to([P, S, K0 * DH0]),
                                ALU.add).then_inc(vs_ready, 1)

            pipelined(e, NBLK, 4, body)


def attend0(nc, qk_hi, qk_lo, v0, gates, o0, ident, fold):
    units = B * K0
    n_blocks = units * QB
    RA = DH0 + DH0 // 2
    RING = 8
    BANKS, CBANKS = 3, 3
    hi_v, lo_v = (a.rearrange("r u d n -> u r d n") for a in (qk_hi, qk_lo))
    o0_v = o0.rearrange("u (q s p) d -> (u q) p s d", p=P, s=S)
    by_vector = [x for x in range(KT) if x % 3 == 2]
    by_pool = [x for x in range(KT) if x % 3 != 2]
    NV, NP = len(by_vector) - 1, len(by_pool) - 1

    def additions(tiles, x):
        return max(tiles.index(x), 1)

    with ExitStack() as ctx:
        sb, pb, sem = names(nc, ctx, "attend0")
        qa, ka = sb("qa", [RA, 2, T], F32R), sb("ka", [RA, 2, T], F32R)
        qb, kb = sb("qb", [RA + 1, 2, T], F32R), sb("kb", [RA + 1, 2, T], F32R)
        v = sb("v", [P, 2, KT, DH0])
        gate, scale = sb("gate", [P, units]), sb("scale", [P, units])
        gate_u, scale_u = sb("gate_u", [P, 2]), sb("scale_u", [P, 2])
        ones = sb("ones", [P, 1])
        probs = sb("probs", [P, RING, BLOCK])
        sum_v, sum_p, sums = sb("sum_v", [P, BLOCK]), sb("sum_p", [P, BLOCK]), sb("sums", [P, 2, BLOCK])
        part = sb("part", [P, S, QB])
        peak, row = sb("peak", [P, S]), sb("row", [S, 2, P], F32R)
        u = sb("u", [P, BLOCK])
        inv, factor = sb("inv", [P, S]), sb("factor", [P, S])
        out = sb("out", [P, 2, S, DH0])
        score_ps = pb("score_ps", [P, BANKS, BLOCK])
        chunk_ps = pb("chunk_ps", [P, CBANKS, BLOCK])
        pv_ps, fold_ps = (pb(n, [P, BLOCK]) for n in ("pv_ps", "fold_ps"))
        row_ps = fold_ps[0:S, BLOCK - P:]

        gates_in, consts, scaled, staged = sem("gates_in"), sem("consts"), sem("scaled"), sem("staged")
        unit_in = sem("unit_in", 2)
        chunk_ready, chunk_read = sem("chunk_ready"), sem("chunk_read")
        peaked, peak_turned, row_ready, row_in = sem("peaked"), sem("peak_turned"), sem("row_ready"), sem("row_in", 2)
        scores_ready, exp_done, pv_done = sem("scores_ready"), sem("exp_done"), sem("pv_done")
        added_v, added_p, summed = sem("added_v"), sem("added_p"), sem("summed")
        u_ready, folded, inverted, out_ready, out_stored = (sem("u_ready"), sem("folded"), sem("inverted"),
                                                            sem("out_ready"), sem("out_stored", 2))
        LOADS = 9
        block = ctx.enter_context(nc.Block())

        @block.sync
        def _(e):
            def load(s):
                wait(e, pv_done, (s.b - 1) * QB * KT)
                half, i = DH0 // 2, s.side
                h, l = at_step(hi_v, s.b), at_step(lo_v, s.b)
                for dst, src in ((ka[0:DH0, i], h[1]), (ka[DH0:RA, i], h[1, 0:half]), (qa[0:DH0, i], h[0]),
                                 (qa[DH0:RA, i], l[0, 0:half]), (qb[0:half, i], l[0, half:DH0]), (qb[half:RA, i], h[0]),
                                 (kb[0:half, i], h[1, half:DH0]), (kb[half:RA, i], l[1])):
                    e.dma_start(dst.bitcast(F32), src).then_inc(unit_in[i], 16)
                e.dma_start(v[:, i], at_step(v0, s.b)).then_inc(unit_in[i], 16)

            def body(at):
                first, mid, prev = at(4), at(1), at(-1)
                if first is not None and first.q == 0:
                    load(first)
                if mid is not None:
                    e.wait_ge(row_ready, mid.t + 1)
                    e.dma_start(qb[RA:RA + 1, mid.side, mid.q * BLOCK:(mid.q + 1) * BLOCK].bitcast(F32)
                                .rearrange("o (s p) -> o s p", s=S), row[:, mid.slot].bitcast(F32)).then_inc(row_in[mid.slot], 16)
                if prev is not None:
                    e.wait_ge(out_ready, prev.t + 1)
                    e.dma_start(at_step(o0_v, prev.t), out[:, prev.slot]).then_inc(out_stored[prev.slot], 16)

            e.dma_start(gate[:], gates.partition_broadcast(P)).then_inc(gates_in, 16)
            pipelined(e, n_blocks, 2 * QB, body, ahead=4)
            for slot in range(2):
                e.wait_ge(out_stored[slot], 16 * n_blocks // 2)

        before = [x - BANKS if x >= BANKS else max(y for y in range(KT) if y % BANKS == x) - KT for x in range(KT)]
        chunk_before = [x - CBANKS if x >= CBANKS else max(y for y in range(KT) if y % CBANKS == x) - KT for x in range(KT)]
        beside = [1] * 13 + [0] * 3
        rest = KT - sum(beside)

        @block.tensor
        def _(e):
            e.wait_ge(consts, 2)

            def chunk(s, x):
                j, kc = x // QB, x % QB
                if x == 0:
                    e.wait_ge(unit_in[s.side], (s.uses + 1) * 16 * LOADS)
                wait(e, chunk_read, s.t * KT + chunk_before[x] + 1)
                e.matmul(chunk_ps[:, x % CBANKS], qa[:, s.side, s.q * BLOCK + j * P:s.q * BLOCK + (j + 1) * P],
                         ka[:, s.side, kc * BLOCK:(kc + 1) * BLOCK], start=True, stop=True).then_inc(chunk_ready, 1)

            def pv(s, x):
                if x == 0:
                    wait(e, u_ready, s.t)
                e.wait_ge(exp_done, s.t * KT + x + 1)
                half = slice(x % 2 * DH0, x % 2 * DH0 + DH0)
                e.matmul(pv_ps[half, :], v[:, s.side, x], probs[:, x % RING], start=(x < 2), stop=(x >= KT - 2))\
                    .then_inc(pv_done, 1)

            def finish(s, j, rows):
                if j == 0:
                    e.wait_ge(u_ready, s.t + 1)
                    e.wait_ge(summed, s.t + 1)
                    wait(e, out_ready, s.t)
                    e.wait_ge(row_ready, rows)
                e.matmul(fold_ps[:, j * DH0:(j + 1) * DH0], u[:, j * P:(j + 1) * P], fold, start=True, stop=True)
                e.matmul(fold_ps[:, S * DH0 + j:S * DH0 + j + 1], sums[:, s.slot, j * P:(j + 1) * P], ones[:],
                         start=True, stop=True).then_inc(folded, 1)

            def body(at):
                far, mid, cur, prev = at(2), at(1), at(0), at(-1)
                c = 0
                for x in range(KT):
                    if cur is not None:
                        if x == 0:
                            e.wait_ge(row_in[cur.slot], (cur.turn + 1) * 16)
                        wait(e, exp_done, cur.t * KT + before[x] + 1)
                        for half, (k_, q_) in enumerate(((ka, qa), (kb, qb))):
                            mm = e.matmul(score_ps[:, x % BANKS], k_[:, cur.side, x * P:(x + 1) * P],
                                          q_[:, cur.side, cur.q * BLOCK:(cur.q + 1) * BLOCK], start=(half == 0), stop=(half == 1))
                        mm.then_inc(scores_ready, 1)
                    if far is not None:
                        for _ in range(beside[x]):
                            chunk(far, c)
                            c += 1
                    if mid is not None and x == 1:
                        e.wait_ge(peaked, mid.t + 1)
                        wait(e, row_ready, mid.t)
                        wait(e, out_ready, mid.t - 2)
                        e.transpose(row_ps, peak[:], ident).then_inc(peak_turned, 1)
                    if cur is not None and x % 2 == 1 and x >= 3:
                        pv(cur, x - 3)
                        pv(cur, x - 2)
                    if prev is not None and 4 <= x < 4 + S:
                        finish(prev, x - 4, n_blocks if mid is None else mid.t + 1)
                if far is not None:
                    for _ in range(rest):
                        chunk(far, c)
                        c += 1
                if cur is not None:
                    pv(cur, KT - 2)
                    pv(cur, KT - 1)

            pipelined(e, n_blocks, 2 * QB, body, ahead=2)

        @block.scalar
        def _(e):
            def body(at):
                s = at(0)
                if s is None:
                    return
                if s.q == 0:
                    e.wait_ge(staged, (s.b + 1) * 2)
                for x in range(KT):
                    e.wait_ge(scores_ready, s.t * KT + x + 1)
                    old, back = (s.t, x - RING) if x >= RING else (s.t - 1, x - RING + KT)
                    wait(e, pv_done, s.t * KT + x - RING + 1)
                    tiles, sem_, n = (by_vector, added_v, NV) if back in by_vector else (by_pool, added_p, NP)
                    wait(e, sem_, old * n + additions(tiles, back))
                    e.activation(probs[:, x % RING], score_ps[:, x % BANKS], ACT.Exp,
                                 scale=scale_u[:, s.side:s.side + 1]).then_inc(exp_done, 1)
                e.wait_ge(pv_done, (s.t + 1) * KT)
                wait(e, folded, s.t * S)
                e.activation(u[:], pv_ps[:], ACT.Copy).then_inc(u_ready, 1)

            pipelined(e, n_blocks, 2 * QB, body, ahead=0, behind=1)

        @block.gpsimd
        def _(e):
            def body(at):
                s = at(0)
                if s is None:
                    return
                for m in range(1, len(by_pool)):
                    x = by_pool[m]
                    e.wait_ge(exp_done, s.t * KT + x + 1)
                    if m == 1:
                        wait(e, summed, s.t)
                        a = probs[:, by_pool[0] % RING]
                    else:
                        e.wait_ge(added_p, s.t * NP + m - 1)
                        a = sum_p[:]
                    e.tensor_tensor(sum_p[:], a, probs[:, x % RING], ALU.add).then_inc(added_p, 1)

            pipelined(e, n_blocks, 2 * QB, body, ahead=0, behind=1)

        @block.vector
        def _(e):
            e.memset(ones[:], 1.0).then_inc(consts, 1)
            e.memset(kb[RA:RA + 1].bitcast(F32), 1.0).then_inc(consts, 1)
            e.wait_ge(gates_in, 16)
            e.tensor_scalar(scale[:], gate[:], DH0 ** -0.5, None, ALU.mult).then_inc(scaled, 1)
            e.wait_ge(scaled, 1)
            e.tensor_tensor(scale[:], scale[:], gate[:], ALU.mult).then_inc(scaled, 1)
            e.wait_ge(scaled, 2)

            def read(s, x):
                e.wait_ge(chunk_ready, s.t * KT + x + 1)
                if x == 0:
                    wait(e, peaked, s.t)
                e.tensor_reduce(part[:, x // QB, x % QB:x % QB + 1], chunk_ps[:, x % CBANKS], AX.X, ALU.max).then_inc(chunk_read, 1)

            def add(s, x):
                m = by_vector.index(x)
                if m == 0:
                    return
                e.wait_ge(exp_done, s.t * KT + x + 1)
                if m == 1:
                    wait(e, summed, s.t)
                    a = probs[:, by_vector[0] % RING]
                else:
                    e.wait_ge(added_v, s.t * NV + m - 1)
                    a = sum_v[:]
                e.tensor_tensor(sum_v[:], a, probs[:, x % RING], ALU.add).then_inc(added_v, 1)

            def total(s):
                e.wait_ge(added_p, (s.t + 1) * NP)
                e.wait_ge(added_v, (s.t + 1) * NV)
                wait(e, folded, (s.t - 1) * S)
                e.tensor_tensor(sums[:, s.slot], sum_v[:], sum_p[:], ALU.add).then_inc(summed, 1)

            def normalise(s):
                e.wait_ge(folded, (s.t + 1) * S)
                e.reciprocal(inv[:], fold_ps[:, S * DH0:S * DH0 + S]).then_inc(inverted, 1)
                e.wait_ge(inverted, s.t * 2 + 1)
                e.tensor_scalar(factor[:], inv[:], gate_u[:, s.side:s.side + 1], None, ALU.mult).then_inc(inverted, 1)
                e.wait_ge(inverted, s.t * 2 + 2)
                wait(e, out_stored[s.slot], s.turn * 16)
                e.tensor_tensor(out[:, s.slot], fold_ps[:, 0:S * DH0].rearrange("p (s d) -> p s d", s=S),
                                factor[:].unsqueeze(2).broadcast_to([P, S, DH0]), ALU.mult).then_inc(out_ready, 1)

            def body(at):
                far, mid, cur, prev = at(2), at(1), at(0), at(-1)
                c = 0
                if mid is not None and mid.q == 0:
                    wait(e, exp_done, (mid.b - 1) * QB * KT)
                    e.tensor_copy(scale_u[:, mid.side:mid.side + 1], scale[:, bass.ds(mid.b, 1)]).then_inc(staged, 1)
                    e.tensor_copy(gate_u[:, mid.side:mid.side + 1], gate[:, bass.ds(mid.b, 1)]).then_inc(staged, 1)
                for x in range(KT):
                    if far is not None:
                        for _ in range(beside[x]):
                            read(far, c)
                            c += 1
                    if mid is not None and x == 2:
                        e.wait_ge(peak_turned, mid.t + 1)
                        wait(e, row_in[mid.slot], mid.turn * 16)
                        e.tensor_copy(row[:, mid.slot], row_ps).then_inc(row_ready, 1)
                    if cur is not None and x - 3 in by_vector:
                        add(cur, x - 3)
                    if prev is not None and x == 1:
                        total(prev)
                    if prev is not None and x == 9:
                        normalise(prev)
                if far is not None:
                    for _ in range(rest):
                        read(far, c)
                        c += 1
                    e.wait_ge(chunk_read, (far.t + 1) * KT)
                    wait(e, peak_turned, far.t)
                    e.tensor_reduce(peak[:], part[:], AX.X, ALU.max, negate=True).then_inc(peaked, 1)
                if cur is not None:
                    for x in (KT - 3, KT - 2, KT - 1):
                        if x in by_vector:
                            add(cur, x)

            pipelined(e, n_blocks, 2 * QB, body, ahead=2)


def between(nc, x, o0, yT, W_o0, b_o0, Wq, Wk, Wv, bq, bk, bv, b_o1, W_r, W_k, W_v, mu_r, mu_k, ident, parts1, v1, base):
    x_v = x.rearrange("b (q s p) d -> (b q) p s d", p=P, s=S)
    o0_v = o0.rearrange("(b k) (q s p) d -> b q k p s d", b=B, p=P, s=S)
    yT_v = yT.rearrange("(c p) (t n) -> t p c n", p=P, n=BLOCK)
    parts_v = parts1.rearrange("a r b (o p) (q n) -> b q a r p o n", p=P, n=BLOCK)
    v1_v = v1.rearrange("(b g) p (q s) e -> b q g p s e", b=B, s=S)
    base_v = base.rearrange("(t s p) d -> t p s d", p=P, s=S)
    HV = 2 * DH1
    with ExitStack() as ctx:
        sb, pb, sem = names(nc, ctx, "between")
        wo, wq, wk, wv = (sb(f"w_{n}", [P, C, D]) for n in ("o", "q", "k", "v"))
        natural = sb("natural", [P, 3, C, D])
        turned_w = sb("turned_w", [P, 3, C, D])
        bias = sb("bias", [P, 4])
        mu, nu = sb("mu", [P, 2, C]), sb("nu", [P, 2, C])
        bo0, bo1, bias_v = sb("bo0", [P, D]), sb("bo1", [P, D]), sb("bias_v", [P, D])
        eps = sb("eps", [P, 1])
        xin, oin, yin = sb("xin", [P, 2, S, D]), sb("oin", [P, 2, S, D]), sb("yin", [P, 2, C, BLOCK])
        ot = sb("ot", [P, C, BLOCK])
        x_bias, x2, x2_bias = sb("x_bias", [P, S, D]), sb("x2", [P, S, D]), sb("x2_bias", [P, 2, S, D])
        st, mv = sb("st", [P, S, 6]), sb("mv", [P, S, 2])
        dev, inv = sb("dev", [P, S]), sb("inv", [P, S])
        xn = sb("xn", [P, S, D])
        xs = sb("xs", [P, 2, C, BLOCK + 1])
        share = sb("share", [P, 2, C, BLOCK])
        mix = sb("mix", [P, 2, 2, C, BLOCK])
        parts = sb("parts", [P, 2, 3, 4, BLOCK], BF16)
        left = sb("left", [P, 4, BLOCK])
        relu, act = sb("relu", [P, C, BLOCK]), sb("act", [P, C, BLOCK])
        tanh_r = sb("tanh_r", [P, S, D])
        ff, total = sb("ff", [P, S, D]), sb("total", [P, S, D])
        vs = sb("vs", [P, 2, S, H1, HV])
        turn_ps, x2_ps = pb("turn_ps", [P, C, BLOCK]), pb("x2_ps", [P, S, D])
        even_ps, odd_ps = pb("even_ps", [P, 2, BLOCK]), pb("odd_ps", [P, 2, BLOCK])

        passed = sem("passed")
        weights_in, prepared, w_turned, w_ready = sem("weights_in"), sem("prepared"), sem("w_turned"), sem("w_ready")
        x_in, o_in, y_in = sem("x_in", 2), sem("o_in", 2), sem("y_in", 2)
        o_turned, ot_ready, x2_summed = sem("o_turned"), sem("ot_ready"), sem("x2_summed")
        x_biased, x2_ready, x2_biased = sem("x_biased"), sem("x2_ready"), sem("x2_biased")
        stats, deviation, inverse, normed = sem("stats"), sem("deviation"), sem("inverse"), sem("normed")
        xn_turned, xs_ready, carried = sem("xn_turned"), sem("xs_ready"), sem("carried")
        shared, mixed = sem("shared"), sem("mixed")
        q_ready, k_ready, kf_ready, v_ready, r_ready, vf_ready = (sem(n) for n in (
            "q_ready", "k_ready", "kf_ready", "v_ready", "r_ready", "vf_ready"))
        part_h, rest_h, part_m, part_l = sem("part_h"), sem("rest_h"), sem("part_m"), sem("part_l")
        rectified, squared, squashed = sem("rectified"), sem("squared"), sem("squashed")
        vs_ready, gated, total_ready = sem("vs_ready"), sem("gated"), sem("total_ready")
        parts_out, vs_out, total_out = sem("parts_out", 2), sem("vs_out", 2), sem("total_out")
        WEIGHTS = 4 + 3 + 2 + 2 + 3
        block = ctx.enter_context(nc.Block())

        @block.sync
        def _(e):
            for w, v in ((wo, W_o0), (wq, Wq), (wk, Wk), (wv, Wv)):
                e.dma_start(w[:], v.rearrange("(c p) h -> p c h", p=P)).then_inc(weights_in, 16)
            for n, v in enumerate((W_r, W_k, W_v)):
                e.dma_start(natural[:, n], v.rearrange("(o p) c -> p o c", p=P)).then_inc(weights_in, 16)
            for n, v in enumerate((bq, bk)):
                e.dma_start(bias[:, 2 * n:2 * n + 2], v.rearrange("(c p) -> p c", p=P), allow_slow_non_contiguous=True)\
                    .then_inc(weights_in, 16)
            for n, v in enumerate((mu_r, mu_k)):
                e.dma_start(mu[:, n], v.rearrange("(c p) -> p c", p=P), allow_slow_non_contiguous=True).then_inc(weights_in, 16)
            for w, v in ((bo0, b_o0), (bo1, b_o1), (bias_v, bv)):
                e.dma_start(w[:], v.partition_broadcast(P)).then_inc(weights_in, 16)

            def body(at):
                nxt, cur = at(2), at(0)
                if nxt is not None:
                    s = nxt
                    wait(e, x_biased, s.t - 1)
                    e.dma_start(xin[:, s.slot], at_step(x_v, s.t)).then_inc(x_in[s.slot], 16)
                    wait(e, o_turned, s.t - 1)
                    for k in range(K0):
                        e.dma_start(oin[:, s.slot, :, k * DH0:(k + 1) * DH0], at_step(o0_v, s.b)[s.q, k]).then_inc(o_in[s.slot], 16)
                    wait(e, x2_summed, s.t - 1)
                    e.dma_start(yin[:, s.slot], at_step(yT_v, s.t)).then_inc(y_in[s.slot], 16)
                if cur is not None:
                    s = cur
                    e.wait_ge(part_m, (s.t + 1) * 4)
                    e.wait_ge(part_l, (s.t + 1) * 4)
                    for a in range(3):
                        for r in range(2):
                            e.dma_start(at_step(parts_v, s.b)[s.q, a, r], parts[:, s.slot, a, 2 * r:2 * r + 2])\
                                .then_inc(parts_out[s.slot], 16)
                    e.wait_ge(vs_ready, s.t + 1)
                    for g in range(H1 // G1):
                        e.dma_start(at_step(v1_v, s.b)[s.q, g],
                                    vs[:, s.slot, :, g * G1:(g + 1) * G1].rearrange("p s h e -> p s (h e)")).then_inc(vs_out[s.slot], 16)
                    e.wait_ge(total_ready, s.t + 1)
                    e.dma_start(at_step(base_v, s.t), total[:]).then_inc(total_out, 16)

            pipelined(e, NBLK, 4, body, ahead=2)
            for slot in range(2):
                e.wait_ge(parts_out[slot], 16 * 6 * NBLK // 2)
                e.wait_ge(vs_out[slot], 16 * (H1 // G1) * NBLK // 2)
            e.wait_ge(total_out, 16 * NBLK)

        @block.tensor
        def _(e):
            e.wait_ge(weights_in, 16 * WEIGHTS)
            for n in range(3):
                if n > 0:
                    e.wait_ge(w_ready, n)
                for c in range(C):
                    for o in range(C):
                        mm = e.transpose(turn_ps[:, c, o * P:(o + 1) * P], natural[:, n, o, c * P:(c + 1) * P], ident)
                mm.then_inc(w_turned, 1)
            e.wait_ge(w_ready, 3)

            def columns(out, w, rhs, ready):
                for o in range(C):
                    for c in range(C):
                        mm = e.matmul(out[:, o], w[:, c, o * P:(o + 1) * P], rhs[:, c], start=(c == 0), stop=(c == C - 1))
                    mm.then_inc(ready, 1)

            def tokens(out, lhs, w, ready):
                out = out[:].rearrange("p a (b d) -> p (a b) d", d=D)
                for j in range(S):
                    for c in range(C):
                        mm = e.matmul(out[:, j], lhs[:, c, j * P:(j + 1) * P], w[:, c], start=(c == 0), stop=(c == C - 1))
                mm.then_inc(ready, 1)

            def body(at):
                nxt, cur = at(1), at(0)
                if nxt is not None:
                    s = nxt
                    e.wait_ge(o_in[s.slot], (s.turn + 1) * 16 * K0)
                    wait(e, xs_ready, s.t * C)
                    for j in range(S):
                        for c in range(C):
                            mm = e.transpose(turn_ps[:, c, j * P:(j + 1) * P], oin[:, s.slot, j, c * P:(c + 1) * P], ident)
                    mm.then_inc(o_turned, 1)
                if cur is not None:
                    s, t = cur, cur.t
                    now = xs[:, s.slot, :, 1:]
                    e.wait_ge(xs_ready, (t + 1) * C)
                    wait(e, squashed, t)
                    columns(even_ps, wq, now, q_ready)
                if nxt is not None:
                    s = nxt
                    e.wait_ge(ot_ready, (s.t + 1) * C)
                    e.wait_ge(y_in[s.slot], (s.turn + 1) * 16)
                    wait(e, x2_ready, s.t)
                    for j in range(S):
                        for c in range(C):
                            e.matmul(x2_ps[:, j], ot[:, c, j * P:(j + 1) * P], wo[:, c], start=(c == 0), stop=False,
                                     skip_group_check=True)
                        for c in range(C):
                            mm = e.matmul(x2_ps[:, j, c * P:(c + 1) * P], yin[:, s.slot, c, j * P:(j + 1) * P], ident,
                                          start=False, stop=(c == C - 1), skip_group_check=True)
                    mm.then_inc(x2_summed, 1)
                if cur is not None:
                    s, t = cur, cur.t
                    wait(e, gated, t)
                    columns(odd_ps, wk, now, k_ready)
                    e.wait_ge(rest_h, t * 4 + 2)
                    e.wait_ge(mixed, (t + 1) * 2 * C)
                    columns(even_ps, turned_w[:, 1], mix[:, s.slot, 1], kf_ready)
                    e.wait_ge(rest_h, t * 4 + 4)
                    tokens(odd_ps, now, wv, v_ready)
                    e.wait_ge(rectified, t + 1)
                    tokens(even_ps, mix[:, s.slot, 0], turned_w[:, 0], r_ready)
                if nxt is not None:
                    s = nxt
                    e.wait_ge(normed, (s.t + 1) * S)
                    for j in range(S):
                        for c in range(C):
                            mm = e.transpose(turn_ps[:, c, j * P:(j + 1) * P], xn[:, j, c * P:(c + 1) * P], ident)
                    mm.then_inc(xn_turned, 1)
                if cur is not None:
                    e.wait_ge(squared, cur.t + 1)
                    e.wait_ge(vs_ready, cur.t + 1)
                    tokens(odd_ps, act, turned_w[:, 2], vf_ready)

            pipelined(e, NBLK, 4, body)

        @block.scalar
        def _(e):
            for n in range(3):
                e.wait_ge(w_turned, n + 1)
                e.activation(turned_w[:, n], turn_ps[:, :, 0:D], ACT.Copy).then_inc(w_ready, 1)
            e.wait_ge(prepared, 3)

            def body(at):
                nxt, cur = at(1), at(0)
                if nxt is not None:
                    e.wait_ge(o_turned, nxt.t + 1)
                    wait(e, x2_summed, nxt.t)
                    for c in range(C):
                        e.activation(ot[:, c], turn_ps[:, c], ACT.Copy).then_inc(ot_ready, 1)
                if cur is not None:
                    s, t = cur, cur.t
                    wait(e, parts_out[s.slot], s.turn * 16 * 6)
                    for o in range(4):
                        if o < 2:
                            e.wait_ge(q_ready, t * 2 + o + 1)
                        else:
                            e.wait_ge(k_ready, t * 2 + o - 1)
                        src = (even_ps, odd_ps)[o // 2][:, o % 2]
                        e.activation(parts[:, s.slot, 0, o], src, ACT.Identity, bias=bias[:, o:o + 1]).then_inc(part_h, 1)
                    e.wait_ge(kf_ready, (t + 1) * 2)
                    wait(e, squared, t)
                    e.activation(relu[:], even_ps[:], ACT.Relu).then_inc(rectified, 1)
                if nxt is not None:
                    e.wait_ge(stats, (nxt.t + 1) * 2 * S)
                    e.activation(dev[:], mv[:, :, 1], ACT.Sqrt, bias=eps[:, 0:1]).then_inc(deviation, 1)
                if cur is not None:
                    e.wait_ge(r_ready, cur.t + 1)
                    wait(e, gated, cur.t)
                    e.activation(tanh_r[:], even_ps[:].rearrange("p a (b d) -> p (a b) d", d=D), ACT.Tanh, scale=0.5)\
                        .then_inc(squashed, 1)
                if nxt is not None:
                    s = nxt
                    e.wait_ge(xn_turned, s.t + 1)
                    wait(e, v_ready, s.t - 1)
                    wait(e, mixed, (s.t - 1) * 2 * C)
                    wait(e, carried, s.t)
                    for c in range(C):
                        e.activation(xs[:, s.slot, c, 1:], turn_ps[:, c], ACT.Copy).then_inc(xs_ready, 1)

            pipelined(e, NBLK, 4, body)

        @block.gpsimd
        def _(e):
            e.memset(eps[:], EPS).then_inc(prepared, 1)
            e.memset(vs[:], 1.0).then_inc(prepared, 1)
            e.wait_ge(weights_in, 16 * WEIGHTS)

            def body(at):
                nxt, cur = at(1), at(0)
                if nxt is not None:
                    s = nxt
                    e.wait_ge(x_in[s.slot], (s.turn + 1) * 16)
                    wait(e, x2_ready, s.t)
                    e.tensor_tensor(x_bias[:], xin[:, s.slot], bo0[:].unsqueeze(1).broadcast_to([P, S, D]), ALU.add)\
                        .then_inc(x_biased, 1)
                if cur is not None:
                    s, t = cur, cur.t
                    wait(e, parts_out[s.slot], s.turn * 16 * 6)
                    for o in range(4):
                        e.wait_ge(part_m, t * 4 + o + 1)
                        e.tensor_tensor(parts[:, s.slot, 2, o], left[:, o], parts[:, s.slot, 1, o], ALU.subtract).then_inc(part_l, 1)
                    e.wait_ge(rectified, t + 1)
                    wait(e, vf_ready, t)
                    e.tensor_tensor(act[:], relu[:], relu[:], ALU.mult).then_inc(squared, 1)
                if nxt is not None:
                    s = nxt
                    e.wait_ge(x2_ready, s.t + 1)
                    wait(e, total_ready, s.t - 1)
                    e.tensor_tensor(x2_bias[:, s.slot], x2[:], bo1[:].unsqueeze(1).broadcast_to([P, S, D]), ALU.add)\
                        .then_inc(x2_biased, 1)

            pipelined(e, NBLK, 4, body)

        @block.vector
        def _(e):
            e.wait_ge(weights_in, 16 * WEIGHTS)
            e.tensor_scalar(nu[:], mu[:], -1.0, 1.0, ALU.mult, ALU.add).then_inc(prepared, 1)
            e.wait_ge(prepared, 3)

            def split(s, o):
                t = s.t
                e.wait_ge(part_h, t * 4 + o + 1)
                wait(e, part_l, (t - 1) * 4 + o + 1)
                src = (even_ps, odd_ps)[o // 2][:, o % 2]
                e.scalar_tensor_tensor(out=left[:, o], in0=src, scalar=bias[:, o:o + 1], in1=parts[:, s.slot, 0, o],
                                       op0=ALU.add, op1=ALU.subtract).then_inc(rest_h, 1)
                e.wait_ge(rest_h, t * 4 + o + 1)
                e.tensor_copy(parts[:, s.slot, 1, o], left[:, o]).then_inc(part_m, 1)

            def body(at):
                nxt, cur = at(1), at(0)
                if cur is not None:
                    wait(e, parts_out[cur.slot], cur.turn * 16 * 6)
                    split(cur, 0)
                    split(cur, 1)
                if nxt is not None:
                    s = nxt
                    e.wait_ge(x2_summed, s.t + 1)
                    e.wait_ge(x_biased, s.t + 1)
                    wait(e, x2_biased, s.t)
                    wait(e, normed, s.t * S)
                    e.tensor_tensor(x2[:], x2_ps[:], x_bias[:], ALU.add).then_inc(x2_ready, 1)
                    e.wait_ge(x2_ready, s.t + 1)
                    for j in range(S):
                        e.bn_stats(st[:, j], x2[:, j]).then_inc(stats, 1)
                    e.wait_ge(stats, s.t * 2 * S + S)
                    hold(e, passed)
                    for j in range(S):
                        e.bn_aggr(mv[:, j], st[:, j]).then_inc(stats, 1)
                if cur is not None:
                    split(cur, 2)
                    split(cur, 3)
                    e.wait_ge(v_ready, cur.t + 1)
                    wait(e, vs_out[cur.slot], cur.turn * 16 * (H1 // G1))
                    e.tensor_tensor(vs[:, cur.slot, :, :, 0:DH1],
                                    odd_ps[:].rearrange("p a (b h d) -> p (a b) h d", b=S // 2, h=H1),
                                    bias_v[:].rearrange("p (h d) -> p h d", h=H1).unsqueeze(1).broadcast_to([P, S, H1, DH1]),
                                    ALU.add).then_inc(vs_ready, 1)
                if nxt is not None:
                    s = nxt
                    e.wait_ge(deviation, s.t + 1)
                    e.reciprocal(inv[:], dev[:]).then_inc(inverse, 1)
                    wait(e, xn_turned, s.t)
                    e.wait_ge(inverse, s.t + 1)
                    for j in range(S):
                        e.tensor_scalar(xn[:, j], x2[:, j], mv[:, j, 0:1], inv[:, j:j + 1],
                                        ALU.subtract, ALU.mult).then_inc(normed, 1)
                if cur is not None:
                    s, t = cur, cur.t
                    e.wait_ge(vf_ready, t + 1)
                    e.wait_ge(squashed, t + 1)
                    wait(e, total_ready, t)
                    e.scalar_tensor_tensor(out=ff[:], in0=tanh_r[:], scalar=1.0,
                                           in1=odd_ps[:].rearrange("p a (b d) -> p (a b) d", d=D),
                                           op0=ALU.add, op1=ALU.mult).then_inc(gated, 1)
                    e.wait_ge(gated, t + 1)
                    e.wait_ge(x2_biased, t + 1)
                    wait(e, total_out, t * 16)
                    e.scalar_tensor_tensor(out=total[:], in0=ff[:], scalar=0.5, in1=x2_bias[:, s.slot],
                                           op0=ALU.mult, op1=ALU.add).then_inc(total_ready, 1)
                if nxt is not None:
                    s = nxt
                    wait(e, mixed, (s.t - 1) * 2 * C)
                    wait(e, v_ready, s.t - 1)
                    if s.q == 0:
                        e.memset(xs[:, s.slot, :, 0:1], 0.0).then_inc(carried, 1)
                    else:
                        e.wait_ge(xs_ready, s.t * C)
                        e.tensor_copy(xs[:, s.slot, :, 0:1], xs[:, 1 - s.slot, :, BLOCK:BLOCK + 1]).then_inc(carried, 1)
                    e.wait_ge(carried, s.t + 1)
                    e.wait_ge(xs_ready, (s.t + 1) * C)
                    wait(e, r_ready, s.t - 1)
                    wait(e, mixed, s.t * 2 * C)
                    for n in range(2):
                        if n > 0:
                            e.wait_ge(mixed, s.t * 2 * C + C)
                        for c in range(C):
                            e.tensor_scalar(share[:, n, c], xs[:, s.slot, c, 0:BLOCK], nu[:, n, c:c + 1], None, ALU.mult)\
                                .then_inc(shared, 1)
                        for c in range(C):
                            e.wait_ge(shared, (s.t * 2 + n) * C + c + 1)
                            e.scalar_tensor_tensor(out=mix[:, s.slot, n, c], in0=xs[:, s.slot, c, 1:],
                                                   scalar=mu[:, n, c:c + 1], in1=share[:, n, c],
                                                   op0=ALU.mult, op1=ALU.add).then_inc(mixed, 1)

            pipelined(e, NBLK, 4, body)


def attend1(nc, parts1, v1, o1, ident, upper):
    units = B * H1 // G1
    R = 6 * DH1
    Q_PARTS, K_PARTS = (0, 0, 1, 0, 2, 1), (0, 1, 0, 2, 0, 1)
    HV = 2 * DH1
    RING, BANKS, LEAD = 16, 3, 80
    CBANKS = 3
    GROUPS = [(q, kt) for q in range(QB) for kt in range(S * (q + 1))]
    NG = len(GROUPS)
    N = NG * G1
    LAST = [max(g for g in range(NG) if GROUPS[g][0] == q) for q in range(QB)]
    CHUNKS = [(q, j, h, kc) for q in range(QB) for j in range(S) for h in range(G1) for kc in range(q + 1)]
    assert len(CHUNKS) == N and NG % 2 == 0
    CHUNK_END = [(LAST[q] + 1) * G1 for q in range(QB)]

    def after_block(g, lag):
        return [(d, q) for d in (-1, 0) for q in range(QB) if LAST[q] + lag == g - d * NG]

    def after_maxima(g, lag):
        return [(d, q) for d in (0, 1) for q in range(QB) if (CHUNK_END[q] - LEAD) // G1 - 1 + lag == g - d * NG]

    def chunk_at(x):
        return (0, x + LEAD) if x + LEAD < N else (1, x + LEAD - N)

    MASKED = [sum(1 for q, kt in GROUPS[:g + 1] if kt >= S * q) * G1 for g in range(NG)]

    def same_bank_before(x, banks):
        return x - banks if x >= banks else max(y for y in range(N) if y % banks == x) - N

    before, chunk_before = ([same_bank_before(x, banks) for x in range(N)] for banks in (BANKS, CBANKS))

    def turns_before(at, g, after, lag):
        t = [at(d).t - d for d in (-1, 0, 1) if at(d) is not None][0]
        ahead = sum(1 for x in range(g) for d, _ in after(x, lag) if d == 1)
        own = sum(1 for x in range(g) for d, _ in after(x, lag) if d == 0)
        behind = sum(1 for x in range(g, NG) for d, _ in after(x, lag) if d == -1)
        early = sum(1 for x in range(NG) for d, _ in after(x, lag) if d == 1)
        number = t * QB - behind + own + early + ahead
        return min(number, units * QB) if isinstance(number, int) else number
    parts_v = parts1.rearrange("a r b (g h d) n -> (b g) a r d h n", g=H1 // G1, h=G1)
    o1_v = o1.rearrange("u (q s p) e -> u q p s e", p=P, s=S)

    with ExitStack() as ctx:
        sb, pb, sem = names(nc, ctx, "attend1")
        qs, ks = sb("qs", [R + 1, 2, G1, T], BF16), sb("ks", [R + 1, 2, G1, T], BF16)
        v = sb("v", [P, 2, KT, G1 * HV])
        probs = sb("probs", [P, RING, BLOCK])
        part = sb("part", [P, G1, S, 1 + QB - 1])
        masked_out = sb("masked_out", [P, 2, BLOCK])
        peak, row = sb("peak", [P, G1 * S]), sb("row", [G1 * S, 2, P], BF16)
        u, inv = sb("u", [P, BLOCK]), sb("inv", [P, S, G1])
        out = sb("out", [P, 2, S, G1, DH1])
        score_ps, chunk_ps = pb("score_ps", [P, BANKS, BLOCK]), pb("chunk_ps", [P, CBANKS, BLOCK])
        pv_ps, turn_ps = (pb(n, [P, BLOCK]) for n in ("pv_ps", "turn_ps"))

        consts, unit_in = sem("consts"), sem("unit_in", 2)
        passed, pool_passed = sem("passed"), sem("pool_passed")
        chunk_ready, chunk_read = sem("chunk_ready"), sem("chunk_read")
        peaked, peak_turned, row_ready, row_in = sem("peaked"), sem("peak_turned"), sem("row_ready"), sem("row_in", 2)
        scores_ready, exp_done, masked, pv_done = sem("scores_ready"), sem("exp_done"), sem("masked"), sem("pv_done")
        u_ready, u_turned, inverted, out_ready, out_stored = (sem("u_ready"), sem("u_turned"), sem("inverted"),
                                                              sem("out_ready"), sem("out_stored", 2))
        LOADS = 2 * 6 + 1
        block = ctx.enter_context(nc.Block())

        @block.sync
        def _(e):
            def load(s):
                wait(e, pv_done, (s.t - 1) * NG)
                for r, (tile, order) in enumerate(((qs, Q_PARTS), (ks, K_PARTS))):
                    for n, a in enumerate(order):
                        e.dma_start(tile[n * DH1:(n + 1) * DH1, s.slot], at_step(parts_v, s.t)[a, r]).then_inc(unit_in[s.slot], 16)
                e.dma_start(v[:, s.slot], at_step(v1, s.t)).then_inc(unit_in[s.slot], 16)

            def body(at):
                if at(1) is not None:
                    load(at(1))
                for g in range(NG):
                    for d, q in after_maxima(g, 2):
                        s = at(d)
                        if s is not None:
                            e.wait_ge(row_ready, s.t * QB + q + 1)
                            for h in range(G1):
                                e.dma_start(qs[R:R + 1, s.slot, h, q * BLOCK:(q + 1) * BLOCK].rearrange("o (s p) -> o s p", s=S),
                                            row[h * S:(h + 1) * S, q % 2]).then_inc(row_in[q % 2], 16)
                    for d, q in after_block(g, 4):
                        s = at(d)
                        if s is not None:
                            e.wait_ge(out_ready, s.t * QB + q + 1)
                            e.dma_start(at_step(o1_v, s.t)[q],
                                        out[:, q % 2].rearrange("p s h d -> p s (h d)")).then_inc(out_stored[q % 2], 16)

            pipelined(e, units, 2, body)
            for n in range(2):
                e.wait_ge(out_stored[n], 16 * units * QB // 2)

        @block.tensor
        def _(e):
            e.wait_ge(consts, 1)

            def chunk(s, n):
                q, j, h, kc = CHUNKS[n]
                if n == 0:
                    e.wait_ge(unit_in[s.slot], (s.turn + 1) * 16 * LOADS)
                wait(e, chunk_read, s.t * N + chunk_before[n] + 1)
                width = BLOCK if kc < q else (j + 1) * P
                tile = q * BLOCK + j * P
                e.matmul(chunk_ps[:, n % CBANKS, 0:width], qs[0:R, s.slot, h, tile:tile + P],
                         ks[0:R, s.slot, h, kc * BLOCK:kc * BLOCK + width], start=True, stop=True).then_inc(chunk_ready, 1)

            def pv(s, g):
                q, kt = GROUPS[g]
                if kt == 0:
                    wait(e, u_ready, s.t * QB + q)
                e.wait_ge(exp_done, s.t * N + (g + 1) * G1)
                if kt >= S * q:
                    e.wait_ge(masked, s.t * MASKED[-1] + MASKED[g])
                off = max(0, kt - S * q) * P
                for h in range(G1):
                    mm = e.matmul(pv_ps[h * HV:(h + 1) * HV, off:], v[:, s.slot, kt, h * HV:(h + 1) * HV],
                                  probs[:, (g * G1 + h) % RING, off:], start=(kt == 0), stop=(g == LAST[q]))
                mm.then_inc(pv_done, 1)

            def body(at):
                cur = at(0)
                for g in range(NG):
                    q, kt = GROUPS[g]
                    off = max(0, kt - S * q) * P
                    for what, h in (("score", 0), ("chunk", 0), ("score", 1), ("score", 2), ("chunk", 1), ("score", 3),
                                    ("chunk", 2), ("turn", 0), ("pv", 0), ("chunk", 3)):
                        x = g * G1 + h
                        if what == "score" and cur is not None:
                            if kt == 0 and h == 0:
                                e.wait_ge(row_in[q % 2], (cur.t * 2 + q // 2 + 1) * 16 * G1)
                            wait(e, exp_done, cur.t * N + before[x] + 1)
                            e.matmul(score_ps[:, x % BANKS, off:], ks[:, cur.slot, h, kt * P:(kt + 1) * P],
                                     qs[:, cur.slot, h, q * BLOCK + off:(q + 1) * BLOCK], start=True, stop=True)\
                                .then_inc(scores_ready, 1)
                        if what == "chunk":
                            d, n = chunk_at(x)
                            if at(d) is not None and (d == 1 or cur is not None):
                                chunk(at(d), n)
                        if what == "turn":
                            for d, q_ in after_maxima(g, 1):
                                s = at(d)
                                if s is not None:
                                    e.wait_ge(peaked, s.t * QB + q_ + 1)
                                    wait(e, row_ready, s.t * QB + q_)
                                    wait(e, out_ready, turns_before(at, g, after_block, 3))
                                    e.transpose(turn_ps[0:G1 * S, 0:P], peak[:], ident).then_inc(peak_turned, 1)
                        if what == "pv" and g == 0 and at(-1) is not None:
                            pv(at(-1), NG - 1)
                        if what == "pv" and g > 0 and cur is not None:
                            pv(cur, g - 1)
                    for d, q_ in after_block(g, 3):
                        s = at(d)
                        if s is not None:
                            e.wait_ge(u_ready, s.t * QB + q_ + 1)
                            wait(e, out_ready, s.t * QB + q_)
                            wait(e, row_ready, turns_before(at, g + 1, after_maxima, 1))
                            for j in range(S):
                                mm = e.transpose(turn_ps[:, j * P:(j + 1) * P], u[:, j * P:(j + 1) * P], ident)
                            mm.then_inc(u_turned, 1)

            pipelined(e, units, 2, body)

        @block.scalar
        def _(e):
            def body(at):
                for g in range(NG):
                    q, kt = GROUPS[g]
                    off = max(0, kt - S * q) * P
                    if at(0) is not None:
                        s = at(0)
                        wait(e, pv_done, s.t * NG + g - RING // G1 + 1)
                        for h in range(G1):
                            x = g * G1 + h
                            e.wait_ge(scores_ready, s.t * N + x + 1)
                            e.activation(probs[:, x % RING, off:], score_ps[:, x % BANKS, off:], ACT.Exp,
                                         scale=DH1 ** -0.5).then_inc(exp_done, 1)
                    for d, q_ in after_block(g, 1):
                        s = at(d)
                        if s is not None:
                            e.wait_ge(pv_done, s.t * NG + LAST[q_] + 1)
                            wait(e, u_turned, s.t * QB + q_)
                            e.activation(u[:], pv_ps[:], ACT.Copy).then_inc(u_ready, 1)

            pipelined(e, units, 2, body)

        @block.gpsimd
        def _(e):
            def body(at):
                s = at(0)
                if s is None:
                    return
                for g in range(NG):
                    q, kt = GROUPS[g]
                    if kt < S * q:
                        continue
                    off = (kt - S * q) * P
                    for h in range(G1):
                        x = g * G1 + h
                        e.wait_ge(exp_done, s.t * N + x + 1)
                        hold(e, pool_passed)
                        tile = probs[:, x % RING, off:off + P]
                        e.affine_select(out=tile, in_=tile, compare_op=ALU.is_ge, fill=0.0, base=0,
                                        pattern=[[1, P]], channel_multiplier=-1).then_inc(masked, 1)

            pipelined(e, units, 2, body)

        @block.vector
        def _(e):
            e.memset(ks[R:R + 1], 1.0).then_inc(consts, 1)

            def read(s, n):
                q, j, h, kc = CHUNKS[n]
                if j == 0 and h == 0 and kc == 0:
                    wait(e, peaked, s.t * QB + q)
                src = chunk_ps[:, n % CBANKS]
                e.wait_ge(chunk_ready, s.t * N + n + 1)
                if kc < q:
                    e.tensor_reduce(part[:, h, j, 1 + kc:2 + kc], src, AX.X, ALU.max).then_inc(chunk_read, 1)
                    return
                wait(e, chunk_read, s.t * N + n - 1)
                hold(e, passed)
                width = (j + 1) * P
                e.tensor_tensor_reduce(masked_out[:, n % 2, 0:width], src[:, 0:width], upper[:, BLOCK - width:], 1.0, LOWEST,
                                       ALU.add, ALU.max, part[:, h, j, 0:1]).then_inc(chunk_read, 1)

            def body(at):
                cur = at(0)
                for g in range(NG):
                    for h in range(G1):
                        d, n = chunk_at(g * G1 + h)
                        if at(d) is not None and (d == 1 or cur is not None):
                            read(at(d), n)
                    for d, q in after_maxima(g, 0):
                        s = at(d)
                        if s is not None:
                            e.wait_ge(chunk_read, s.t * N + CHUNK_END[q])
                            wait(e, peak_turned, s.t * QB + q)
                            e.tensor_reduce(peak[:], part[:, :, :, 0:1 + q].rearrange("p h s n -> p (h s) n"), AX.X, ALU.max,
                                            negate=True).then_inc(peaked, 1)
                    for d, q in after_maxima(g, 2):
                        s = at(d)
                        if s is not None:
                            e.wait_ge(peak_turned, s.t * QB + q + 1)
                            wait(e, row_in[q % 2], (s.t * 2 + q // 2) * 16 * G1)
                            e.tensor_copy(row[:, q % 2], turn_ps[0:G1 * S, 0:P]).then_inc(row_ready, 1)
                    for d, q in after_block(g, 4):
                        s = at(d)
                        if s is not None:
                            e.wait_ge(u_turned, s.t * QB + q + 1)
                            t_ = turn_ps[:].rearrange("p (s h e) -> p s h e", s=S, h=G1)
                            wait(e, out_ready, s.t * QB + q)
                            e.reciprocal(inv[:], t_[:, :, :, DH1]).then_inc(inverted, 1)
                            e.wait_ge(inverted, s.t * QB + q + 1)
                            wait(e, out_stored[q % 2], (s.t * 2 + q // 2) * 16)
                            e.tensor_tensor(out[:, q % 2], t_[:, :, :, 0:DH1],
                                            inv[:].unsqueeze(3).broadcast_to([P, S, G1, DH1]), ALU.mult).then_inc(out_ready, 1)

            pipelined(e, units, 2, body)


def close(nc, o1, base, W_o, out, ident):
    GW = G1 * DH1
    o1_v = o1.rearrange("(b g) (q s p) e -> b q g p s e", b=B, p=P, s=S)
    base_v = base.rearrange("(t s p) d -> t p s d", p=P, s=S)
    out_v = out.rearrange("b (q s p) d -> (b q) p s d", p=P, s=S)
    with ExitStack() as ctx:
        sb, pb, sem = names(nc, ctx, "close")
        wo = sb("wo", [P, C, D])
        oin, bin_ = sb("oin", [P, 2, S, D]), sb("bin", [P, 2, S, D])
        ot, total = sb("ot", [P, 2, C, BLOCK]), sb("total", [P, 2, S, D])
        turn_ps, y_ps = pb("turn_ps", [P, 2, C, BLOCK]), pb("y_ps", [P, 2, S, D])
        weights_in, o_in, base_in = sem("weights_in"), sem("o_in", 2), sem("base_in", 2)
        turned, ot_ready, projected, total_ready, stored = (sem("turned"), sem("ot_ready"), sem("projected"),
                                                            sem("total_ready"), sem("stored", 2))
        block = ctx.enter_context(nc.Block())

        @block.sync
        def _(e):
            e.dma_start(wo[:], W_o.rearrange("(c p) h -> p c h", p=P)).then_inc(weights_in, 16)

            def body(at):
                nxt, cur = at(2), at(0)
                if nxt is not None:
                    s = nxt
                    wait(e, turned, s.t - 1)
                    for g in range(D // GW):
                        e.dma_start(oin[:, s.slot, :, g * GW:(g + 1) * GW], at_step(o1_v, s.b)[s.q, g]).then_inc(o_in[s.slot], 16)
                    wait(e, total_ready, s.t - 1)
                    e.dma_start(bin_[:, s.slot], at_step(base_v, s.t)).then_inc(base_in[s.slot], 16)
                if cur is not None:
                    s = cur
                    e.wait_ge(total_ready, s.t + 1)
                    e.dma_start(at_step(out_v, s.t), total[:, s.slot]).then_inc(stored[s.slot], 16)

            pipelined(e, NBLK, 4, body, ahead=2)
            for slot in range(2):
                e.wait_ge(stored[slot], 16 * NBLK // 2)

        @block.tensor
        def _(e):
            e.wait_ge(weights_in, 16)

            def body(at):
                nxt, cur = at(1), at(0)
                if nxt is not None:
                    s = nxt
                    e.wait_ge(o_in[s.slot], (s.turn + 1) * 16 * (D // GW))
                    wait(e, ot_ready, s.t - 1)
                    for j in range(S):
                        for c in range(C):
                            mm = e.transpose(turn_ps[:, s.slot, c, j * P:(j + 1) * P], oin[:, s.slot, j, c * P:(c + 1) * P], ident)
                    mm.then_inc(turned, 1)
                if cur is not None:
                    s = cur
                    e.wait_ge(ot_ready, s.t + 1)
                    wait(e, total_ready, s.t - 1)
                    for j in range(S):
                        for c in range(C):
                            mm = e.matmul(y_ps[:, s.slot, j], ot[:, s.slot, c, j * P:(j + 1) * P], wo[:, c],
                                          start=(c == 0), stop=(c == C - 1))
                    mm.then_inc(projected, 1)

            pipelined(e, NBLK, 4, body)

        @block.scalar
        def _(e):
            def body(at):
                s = at(0)
                if s is None:
                    return
                e.wait_ge(turned, s.t + 1)
                wait(e, projected, s.t - 1)
                e.activation(ot[:, s.slot], turn_ps[:, s.slot], ACT.Copy).then_inc(ot_ready, 1)

            pipelined(e, NBLK, 4, body)

        @block.vector
        def _(e):
            def body(at):
                s = at(0)
                if s is None:
                    return
                e.wait_ge(projected, s.t + 1)
                e.wait_ge(base_in[s.slot], (s.turn + 1) * 16)
                wait(e, stored[s.slot], s.turn * 16)
                e.tensor_tensor(total[:, s.slot], y_ps[:, s.slot], bin_[:, s.slot], ALU.add).then_inc(total_ready, 1)

            pipelined(e, NBLK, 4, body)


_INS = {
    "L0_attn_x": "x", "L0_attn_Wa": "Wa", "L0_attn_Wx": "Wx", "L0_attn_ba": "ba", "L0_attn_bx": "bx", "L0_attn_Lam": "Lam",
    "L0_ffn_Wq": "Wq0", "L0_ffn_bq": "bq0", "L0_ffn_Wk": "Wk0", "L0_ffn_bk": "bk0", "L0_ffn_Wv": "Wv0", "L0_ffn_bv": "bv0",
    "L0_ffn_Wr": "Wr0", "L0_ffn_br": "br0", "L0_ffn_Wo": "Wo0", "L0_ffn_bo": "bo0",
    "L1_attn_W_q": "Wq1", "L1_attn_b_q": "bq1", "L1_attn_W_k": "Wk1", "L1_attn_b_k": "bk1",
    "L1_attn_W_v": "Wv1", "L1_attn_b_v": "bv1", "L1_attn_W_o": "Wo1", "L1_attn_b_o": "bo1",
    "L1_ffn_W_r": "W_r", "L1_ffn_W_k": "W_k", "L1_ffn_W_v": "W_v", "L1_ffn_mu_r": "mu_r", "L1_ffn_mu_k": "mu_k",
}


def program(nc, out, x, Wa, Wx, ba, bx, Lam, Wq0, bq0, Wk0, bk0, Wv0, bv0, Wr0, br0, Wo0, bo0,
            Wq1, bq1, Wk1, bk1, Wv1, bv1, Wo1, bo1, W_r, W_k, W_v, mu_r, mu_k):
    def dram(name, shape, dt=F32):
        return nc.dram_tensor(name, shape, dt, kind="Internal").ap()

    nc.disable_value_cache = True
    xnT, yT = dram("xnT", (D, B * T)), dram("yT", (D, B * T))
    chosen, gates = dram("chosen", (B * K0,), U32), dram("gates", (B * K0,))
    qk_hi, qk_lo = dram("qk_hi", (2, B * K0, DH0, T)), dram("qk_lo", (2, B * K0, DH0, T))
    v0, o0 = dram("v0", (B * K0, P, KT, DH0)), dram("o0", (B * K0, T, DH0))
    parts1, v1 = dram("parts1", (3, 2, B, D, T), BF16), dram("v1", (B * H1 // G1, P, KT, G1 * 2 * DH1))
    base, o1 = dram("base", (B * T, D)), dram("o1", (B * H1 // G1, T, G1 * DH1))
    with ExitStack() as ctx:
        sb, _, _ = names(nc, ctx, "program")
        ident, fold, upper = sb("ident", [P, P]), sb("fold", [P, DH0]), sb("upper", [P, BLOCK])
        means = sb("means", [P, C, B])
        constants(nc, ident[:], fold[:], upper[:])
        recurrence(nc, x, Wa, Wx, ba, bx, Lam, xnT, yT, means, ident[:])
        route(nc, means, Wr0, br0, chosen, gates)
        project0(nc, xnT, Wq0, Wk0, Wv0, bq0, bk0, bv0, chosen, qk_hi, qk_lo, v0)
        attend0(nc, qk_hi, qk_lo, v0, gates, o0, ident[:], fold[:])
        between(nc, x, o0, yT, Wo0, bo0, Wq1, Wk1, Wv1, bq1, bk1, bv1, bo1, W_r, W_k, W_v, mu_r, mu_k,
                ident[:], parts1, v1, base)
        attend1(nc, parts1, v1, o1, ident[:], upper[:])
        close(nc, o1, base, Wo1, out, ident[:])


def kernel(**inputs):
    import concourse.bacc as bacc
    from concourse.bass_utils import run_bass_kernel_spmd

    nc = bacc.Bacc("TRN2", target_bir_lowering=False, num_devices=1)
    arrays, args = {}, {}
    for name, short in _INS.items():
        a = np.ascontiguousarray(inputs[name])
        arrays[f"in_{name}"] = a
        args[short] = nc.dram_tensor(f"in_{name}", a.shape, mybir.dt.from_np(a.dtype), kind="ExternalInput").ap()
    out = nc.dram_tensor("out", (B, T, D), F32, kind="ExternalOutput").ap()
    program(nc, out, **args)
    return run_bass_kernel_spmd(nc, [arrays], core_ids=[0]).results[0]["out"]
```

```python
from contextlib import ExitStack

import numpy as np

import concourse.bass as bass
from concourse import mybir

ALU = mybir.AluOpType
ACT = mybir.ActivationFunctionType
AX = mybir.AxisListType
F32 = mybir.dt.float32
F32R = mybir.dt.float32r
BF16 = mybir.dt.bfloat16
U32 = mybir.dt.uint32

P = 128
B, T, D = 4, 2048, 256
C = D // P
BLOCK = 512
S = BLOCK // P
QB = T // BLOCK
NBLK = B * QB
KT = T // P
H0, K0, DH0 = 16, 4, 64
H1, DH1 = 16, 16
G1 = 4
EPS = 1e-5
LN8 = float(np.log(np.float32(8.0)))
LOWEST = -3.0e38


class Step:

    def __init__(self, i, k, unroll):
        self.t = i * unroll + k
        self.slot = k % 2
        self.turn = i * (unroll // 2) + k // 2
        self.place = k % 4
        self.stay = i * (unroll // 4) + k // 4
        self.q = k % QB
        self.b = i * (unroll // QB) + k // QB
        self.side = k // QB % 2
        self.uses = i * (unroll // (2 * QB)) + k // (2 * QB)


def pipelined(e, n, unroll, body, ahead=1, behind=1):
    last = n // unroll - 1

    def edge(current):
        def at(d):
            t = current + d
            return Step(t // unroll, t % unroll, unroll) if 0 <= t < n else None
        body(at)

    for t in range(-ahead, unroll + behind):
        edge(t)
    with e.Fori(1, last) as i:
        for k in range(behind, unroll + behind):
            body(lambda d: Step(i, k + d, unroll))
    for t in range(last * unroll + behind, n + behind):
        edge(t)


def wait(e, sem, value):
    if isinstance(value, int) and value <= 0:
        return
    e.wait_ge(sem, value)


def hold(e, passed):
    e.sem_inc(passed, 1)


def names(nc, ctx, phase):
    def sb(name, shape, dt=F32):
        return ctx.enter_context(nc.sbuf_tensor(f"{phase}_{name}", shape, dt))

    def pb(name, shape, dt=F32):
        return ctx.enter_context(nc.psum_tensor(f"{phase}_{name}", shape, dt))

    def sem(name, n=None):
        if n is None:
            return ctx.enter_context(nc.semaphore(f"{phase}_{name}"))
        return [ctx.enter_context(nc.semaphore(f"{phase}_{name}{i}")) for i in range(n)]

    return sb, pb, sem


def tokens_of(tile, t):
    return tile[:, :, t * BLOCK:(t + 1) * BLOCK] if isinstance(t, int) else tile[:, :, bass.ds(t * BLOCK, BLOCK)]


def at_step(view, index):
    return view[bass.ds(index, 1)].squeeze(0) if not isinstance(index, int) else view[index]


def constants(nc, ident, fold, upper):
    with ExitStack() as ctx:
        _, _, sem = names(nc, ctx, "constants")
        cleared, shaped = sem("cleared"), sem("shaped")
        block = ctx.enter_context(nc.Block())

        @block.gpsimd
        def _(e):
            e.memset(ident, 0.0).then_inc(cleared, 1)
            e.memset(fold, 0.0).then_inc(cleared, 1)
            e.memset(upper, 0.0).then_inc(cleared, 1)
            e.wait_ge(cleared, 3)
            e.affine_select(out=ident, in_=ident, compare_op=ALU.not_equal, fill=1.0, base=0,
                            pattern=[[-1, P]], channel_multiplier=1).then_inc(shaped, 1)
            e.affine_select(out=fold, in_=fold, compare_op=ALU.not_equal, fill=1.0, base=0,
                            pattern=[[-1, DH0]], channel_multiplier=1).then_inc(shaped, 1)
            e.affine_select(out=upper[:, BLOCK - P:], in_=upper[:, BLOCK - P:], compare_op=ALU.is_ge, fill=LOWEST, base=0,
                            pattern=[[-1, P]], channel_multiplier=1).then_inc(shaped, 1)
            e.wait_ge(shaped, 3)
            e.affine_select(out=fold, in_=fold, compare_op=ALU.not_equal, fill=1.0, base=-DH0,
                            pattern=[[-1, DH0]], channel_multiplier=1).then_inc(shaped, 1)
            e.wait_ge(shaped, 4)


def recurrence(nc, x, Wa, Wx, ba, bx, Lam, xnT, yT, means, ident, passed):
    x_v = x.rearrange("b (q s p) d -> (b q) p s d", p=P, s=S)
    yT_v = yT.rearrange("(c p) (t n) -> t p c n", p=P, n=BLOCK)
    with ExitStack() as ctx:
        sb, pb, sem = names(nc, ctx, "recurrence")
        wa, wx = sb("wa", [P, C, D]), sb("wx", [P, C, D])
        bias_r, bias_i = sb("bias_r", [P, C]), sb("bias_i", [P, C])
        lam, decay = sb("lam", [P, C]), sb("decay", [P, C])
        eps, quarter = sb("eps", [P, 1]), sb("quarter", [P, 1])
        xin, xn = sb("xin", [P, 2, S, D]), sb("xn", [P, 2, S, D])
        st, mv = sb("st", [P, S, 6]), sb("mv", [P, S, 2])
        dev, inv = sb("dev", [P, S]), sb("inv", [P, S])
        xt = sb("xt", [P, 2, C, BLOCK])
        tanh_r, tanh_i = sb("tanh_r", [P, C, BLOCK]), sb("tanh_i", [P, 2, C, BLOCK])
        at_raw, at = sb("at_raw", [P, C, BLOCK]), sb("at", [P, 2, C, BLOCK])
        at_sq, root = sb("at_sq", [P, C, BLOCK]), sb("root", [P, 2, C, BLOCK])
        drive = sb("drive", [P, C, BLOCK])
        y = sb("y", [P, 2, C, BLOCK])
        turn_ps = pb("turn_ps", [P, C, BLOCK])
        gate_ps = pb("gate_ps", [P, 2, C, BLOCK])
        block_sum, seq_sum = sb("block_sum", [P, C, QB]), sb("seq_sum", [P, C])

        weights_in = sem("weights_in")
        consts, prepared = sem("consts"), sem("prepared")
        x_in = sem("x_in", 2)
        stats, deviation, inverse, normed = sem("stats"), sem("deviation"), sem("inverse"), sem("normed")
        turned, xt_ready = sem("turned"), sem("xt_ready")
        gates_ready, squashed, decayed = sem("gates_ready"), sem("squashed"), sem("decayed")
        clamped, squared, rooted = sem("clamped"), sem("squared"), sem("rooted")
        driven, scanned, summed = sem("driven"), sem("scanned"), sem("summed")
        xt_out, y_out = sem("xt_out", 2), sem("y_out", 2)
        block = ctx.enter_context(nc.Block())

        @block.sync
        def _(e):
            def body(at_):
                load, turned_, prev = at_(3), at_(1), at_(-1)
                if load is not None:
                    s = load
                    wait(e, normed, (s.t - 1) * S)
                    e.dma_start(xin[:, s.slot], at_step(x_v, s.t)).then_inc(x_in[s.slot], 16)
                if turned_ is not None:
                    s = turned_
                    e.wait_ge(xt_ready, (s.t + 1) * C)
                    e.dma_start(tokens_of(xnT, s.t), xt[:, s.slot]).then_inc(xt_out[s.slot], 16)
                if prev is not None:
                    s = prev
                    e.wait_ge(scanned, (s.t + 1) * C)
                    e.dma_start(at_step(yT_v, s.t), y[:, s.slot]).then_inc(y_out[s.slot], 16)

            for w, v in ((wa, Wa), (wx, Wx)):
                e.dma_start(w[:], v.rearrange("(c p) h -> p c h", p=P)).then_inc(weights_in, 16)
            for w, v in ((bias_r, ba), (bias_i, bx), (lam, Lam)):
                e.dma_start(w[:], v.rearrange("(c p) -> p c", p=P), allow_slow_non_contiguous=True).then_inc(weights_in, 16)
            pipelined(e, NBLK, 4, body, ahead=3)
            for slot in range(2):
                e.wait_ge(xt_out[slot], 16 * NBLK // 2)
                e.wait_ge(y_out[slot], 16 * NBLK // 2)

        @block.vector
        def _(e):
            e.memset(eps[:], EPS).then_inc(consts, 1)
            e.memset(quarter[:], 0.25).then_inc(consts, 1)
            e.wait_ge(weights_in, 16 * 5)
            e.tensor_scalar(bias_r[:], bias_r[:], 0.5, None, ALU.mult).then_inc(prepared, 1)
            e.tensor_scalar(bias_i[:], bias_i[:], 0.5, None, ALU.mult).then_inc(prepared, 1)
            e.wait_ge(prepared, 3)
            e.tensor_scalar(decay[:], decay[:], 1.0, None, ALU.add).then_inc(prepared, 1)
            e.wait_ge(prepared, 4)
            e.reciprocal(lam[:], decay[:]).then_inc(prepared, 1)
            e.wait_ge(prepared, 6)
            e.tensor_scalar(decay[:], decay[:], -0.5 * LN8, None, ALU.add).then_inc(prepared, 1)

            def body(at_):
                far, cur, prev = at_(2), at_(0), at_(-1)
                if far is not None:
                    s = far
                    e.wait_ge(x_in[s.slot], (s.turn + 1) * 16)
                    wait(e, normed, s.t * S)
                    for j in range(S):
                        e.bn_stats(st[:, j], xin[:, s.slot, j]).then_inc(stats, 1)
                    e.wait_ge(stats, s.t * 2 * S + S)
                    hold(e, passed)
                    for j in range(S):
                        e.bn_aggr(mv[:, j], st[:, j]).then_inc(stats, 1)
                if prev is not None:
                    s = prev
                    e.wait_ge(squashed, (s.t + 1) * 2 * C)
                    e.wait_ge(xt_ready, (s.t + 1) * C)
                    wait(e, scanned, s.t * C)
                    e.scalar_tensor_tensor(out=drive[:], in0=tanh_i[:, s.slot], scalar=1.0, in1=xt[:, s.slot],
                                           op0=ALU.add, op1=ALU.mult).then_inc(driven, 1)
                if far is not None:
                    s = far
                    e.wait_ge(deviation, s.t + 1)
                    e.reciprocal(inv[:], dev[:]).then_inc(inverse, 1)
                    wait(e, turned, s.t - 1)
                    e.wait_ge(inverse, s.t + 1)
                    for j in range(S):
                        e.tensor_scalar(xn[:, s.slot, j], xin[:, s.slot, j], mv[:, j, 0:1], inv[:, j:j + 1],
                                        ALU.subtract, ALU.mult).then_inc(normed, 1)
                if prev is not None:
                    s = prev
                    e.wait_ge(driven, s.t * 2 + 1)
                    e.wait_ge(rooted, s.t + 1)
                    e.tensor_tensor(drive[:], drive[:], root[:, s.slot], ALU.mult).then_inc(driven, 1)
                    e.wait_ge(driven, s.t * 2 + 2)
                    e.wait_ge(clamped, s.t + 1)
                    wait(e, y_out[s.slot], s.turn * 16)
                    for c in range(C):
                        start = 0.0 if s.q == 0 else y[:, 1 - s.slot, c, BLOCK - 1:BLOCK]
                        e.tensor_tensor_scan(y[:, s.slot, c], at[:, s.slot, c], drive[:, c], start,
                                             ALU.mult, ALU.add).then_inc(scanned, 1)
                if cur is not None:
                    s = cur
                    e.wait_ge(decayed, (s.t + 1) * C)
                    wait(e, scanned, (s.t - 1) * C)
                    wait(e, squared, s.t - 1)
                    e.tensor_scalar(at[:, s.slot], at_raw[:], 1.0, 0.0, ALU.min, ALU.max).then_inc(clamped, 1)

            def sums(s):
                if s is not None and s.q == QB - 1:
                    e.wait_ge(xt_ready, (s.t + 1) * C)
                    e.tensor_reduce(seq_sum[:], block_sum[:], AX.X, ALU.add).then_inc(summed, 1)
                    e.wait_ge(summed, s.b * 2 + 1)
                    e.tensor_copy(means[:, :, bass.ds(s.b, 1)], seq_sum[:].unsqueeze(2)).then_inc(summed, 1)

            def both(at_):
                body(at_)
                sums(at_(1))

            pipelined(e, NBLK, 4, both, ahead=2)

        @block.scalar
        def _(e):
            e.wait_ge(weights_in, 16 * 5)
            e.wait_ge(prepared, 2)
            e.activation(decay[:], lam[:], ACT.Exp, scale=-1.0).then_inc(prepared, 1)
            e.wait_ge(prepared, 5)
            e.activation(decay[:], lam[:], ACT.Ln).then_inc(prepared, 1)
            e.wait_ge(prepared, 7)
            e.wait_ge(consts, 2)

            def body(at_):
                far, nxt, cur, prev = at_(2), at_(1), at_(0), at_(-1)
                if far is not None:
                    e.wait_ge(stats, (far.t + 1) * 2 * S)
                    wait(e, inverse, far.t)
                    e.activation(dev[:], mv[:, :, 1], ACT.Sqrt, bias=eps[:, 0:1]).then_inc(deviation, 1)
                if prev is not None:
                    s = prev
                    e.wait_ge(squared, s.t + 1)
                    wait(e, driven, (s.t - 1) * 2)
                    e.activation(root[:, s.slot], at_sq[:], ACT.Sqrt, bias=quarter[:, 0:1],
                                 scale=-0.25).then_inc(rooted, 1)
                if nxt is not None:
                    s = nxt
                    e.wait_ge(turned, s.t + 1)
                    wait(e, driven, (s.t - 2) * 2 + 1)
                    wait(e, xt_out[s.slot], s.turn * 16)
                    if s.q == 0:
                        wait(e, summed, s.b * 2)
                    for c in range(C):
                        e.activation(xt[:, s.slot, c], turn_ps[:, c], ACT.Identity,
                                     accum_out=block_sum[:, c, s.q:s.q + 1]).then_inc(xt_ready, 1)
                if cur is not None:
                    s = cur
                    wait(e, decayed, s.t * C)
                    for c in range(C):
                        e.wait_ge(gates_ready, s.t * 2 * C + c + 1)
                        e.activation(tanh_r[:, c], gate_ps[:, 0, c], ACT.Tanh, bias=bias_r[:, c:c + 1],
                                     scale=0.5).then_inc(squashed, 1)
                    wait(e, clamped, s.t)
                    for c in range(C):
                        e.wait_ge(squashed, s.t * 2 * C + c + 1)
                        e.activation(at_raw[:, c], tanh_r[:, c], ACT.Exp, bias=decay[:, c:c + 1],
                                     scale=-0.5 * LN8).then_inc(decayed, 1)
                    wait(e, driven, (s.t - 1) * 2)
                    for c in range(C):
                        e.wait_ge(gates_ready, s.t * 2 * C + C + c + 1)
                        e.activation(tanh_i[:, s.slot, c], gate_ps[:, 1, c], ACT.Tanh, bias=bias_i[:, c:c + 1],
                                     scale=0.5).then_inc(squashed, 1)

            pipelined(e, NBLK, 4, body, ahead=2)

        @block.gpsimd
        def _(e):
            def body(at_):
                s = at_(0)
                if s is None:
                    return
                e.wait_ge(clamped, s.t + 1)
                wait(e, rooted, s.t)
                e.tensor_tensor(at_sq[:], at[:, s.slot], at[:, s.slot], ALU.mult).then_inc(squared, 1)

            pipelined(e, NBLK, 4, body)

        @block.tensor
        def _(e):
            e.wait_ge(weights_in, 16 * 5)

            def body(at_):
                nxt, cur = at_(1), at_(0)
                if nxt is not None:
                    s = nxt
                    e.wait_ge(normed, (s.t + 1) * S)
                    wait(e, xt_ready, s.t * C)
                    for j in range(S):
                        for c in range(C):
                            tile = xn[:, s.slot, j, c * P:(c + 1) * P]
                            mm = e.transpose(turn_ps[:, c, j * P:(j + 1) * P], tile, ident)
                    mm.then_inc(turned, 1)
                if cur is not None:
                    s = cur
                    e.wait_ge(xt_ready, (s.t + 1) * C)
                    for g, w in enumerate((wa, wx)):
                        for o in range(C):
                            wait(e, squashed, (s.t - 1) * 2 * C + g * C + o + 1)
                            for c in range(C):
                                mm = e.matmul(gate_ps[:, g, o], w[:, c, o * P:(o + 1) * P], xt[:, s.slot, c],
                                              start=(c == 0), stop=(c == C - 1))
                            mm.then_inc(gates_ready, 1)

            pipelined(e, NBLK, 4, body)


def route(nc, means, Wr, br, chosen, gates):
    with ExitStack() as ctx:
        sb, pb, sem = names(nc, ctx, "route")
        wr, brow = sb("wr", [P, C, H0]), sb("brow", [B, H0])
        logits, weights = sb("logits", [B, H0]), sb("weights", [B, H0])
        top, neg, total = sb("top", [B, 8]), sb("neg", [B, 1]), sb("total", [B, 1])
        best, place = sb("best", [B, 8]), sb("place", [B, 8], U32)
        ex, rest, norm, gate = sb("ex", [B, K0]), sb("rest", [B, 1]), sb("norm", [B, 1]), sb("gate", [B, K0])
        lin = pb("lin", [B, BLOCK])
        loaded, projected, step, exp_done, stored = (sem("loaded"), sem("projected"), sem("step"),
                                                     sem("exp_done"), sem("stored"))
        block = ctx.enter_context(nc.Block())

        @block.sync
        def _(e):
            e.dma_start(wr[:], Wr.rearrange("(c p) h -> p c h", p=P)).then_inc(loaded, 16)
            e.dma_start(brow[:], br.partition_broadcast(B)).then_inc(loaded, 16)
            e.wait_ge(step, 12)
            e.dma_start(chosen.rearrange("(b k) -> b k", k=K0), place[:, 0:K0]).then_inc(stored, 16)
            e.dma_start(gates.rearrange("(b k) -> b k", k=K0), gate[:]).then_inc(stored, 16)
            e.wait_ge(stored, 32)

        @block.tensor
        def _(e):
            e.wait_ge(loaded, 32)
            for c in range(C):
                mm = e.matmul(lin[:, 0:H0], means[:, c, :], wr[:, c, :], start=(c == 0), stop=(c == C - 1))
            mm.then_inc(projected, 1)

        @block.scalar
        def _(e):
            e.wait_ge(step, 3)
            e.activation(weights[:], logits[:], ACT.Exp, bias=neg[:, 0:1], accum_out=total[:]).then_inc(exp_done, 1)
            e.wait_ge(step, 8)
            e.activation(ex[:], best[:, 0:K0], ACT.Exp, bias=neg[:, 0:1], accum_out=norm[:]).then_inc(exp_done, 1)
            e.activation(rest[:], neg[:], ACT.Exp).then_inc(exp_done, 1)

        @block.vector
        def _(e):
            count = [0]

            def link(ins):
                count[0] += 1
                ins.then_inc(step, 1)
                e.wait_ge(step, count[0])

            e.wait_ge(projected, 1)
            link(e.scalar_tensor_tensor(out=logits[:], in0=lin[:, 0:H0], scalar=1.0 / T, in1=brow[:],
                                        op0=ALU.mult, op1=ALU.add))
            link(e.max(top[:], logits[:]))
            link(e.tensor_scalar(neg[:], top[:, 0:1], -1.0, None, ALU.mult))
            e.wait_ge(exp_done, 1)
            link(e.reciprocal(total[:], total[:]))
            link(e.tensor_scalar(weights[:], weights[:], total[:, 0:1], None, ALU.mult))
            link(e.max(best[:], weights[:]))
            link(e.max_index(place[:], best[:], weights[:]))
            link(e.tensor_scalar(neg[:], best[:, 0:1], -1.0, None, ALU.mult))
            e.wait_ge(exp_done, 3)
            link(e.tensor_scalar(rest[:], rest[:], float(H0 - K0), None, ALU.mult))
            link(e.tensor_tensor(norm[:], norm[:], rest[:], ALU.add))
            link(e.reciprocal(norm[:], norm[:]))
            link(e.tensor_scalar(gate[:], ex[:], norm[:, 0:1], None, ALU.mult))


def project0(nc, xnT, Wq, Wk, Wv, bq, bk, bv, chosen, qk_hi, qk_lo, v0, passed):
    hi_v, lo_v = (a.rearrange("r (b o u) d (q n) -> b q r (u d) o n", b=B, o=2, n=BLOCK) for a in (qk_hi, qk_lo))
    v0_v = v0.rearrange("b p (q s) e -> b q p s e", s=S)
    with ExitStack() as ctx:
        sb, pb, sem = names(nc, ctx, "project0")
        picks = sb("picks", [1, B * K0], U32)
        stage = sb("stage", [P, 3, C, K0 * DH0])
        stage_bias, stage_bias_v = sb("stage_bias", [P, 4]), sb("stage_bias_v", [P, K0 * DH0])
        w_hi, w_lo = (sb(n, [P, 3, C, K0 * DH0], F32R) for n in ("w_hi", "w_lo"))
        bias = sb("bias", [P, 4])
        bias_v = sb("bias_v", [P, K0 * DH0])
        x_hi, x_lo = sb("x_hi", [P, 2, C, BLOCK], F32R), sb("x_lo", [P, 2, C, BLOCK], F32R)
        hi, lo = sb("hi", [P, 2, 4, BLOCK], F32R), sb("lo", [P, 2, 4, BLOCK], F32R)
        vs = sb("vs", [P, 2, S, K0 * DH0])
        qk_ps = pb("qk_ps", [P, 4, BLOCK])
        v_ps = pb("v_ps", [P, S, K0 * DH0])

        picks_in, staged = sem("picks_in"), sem("staged")
        w_hi_ready, w_lo_ready, bias_ready = sem("w_hi_ready"), sem("w_lo_ready"), sem("bias_ready")
        x_hi_ready, x_lo_ready = sem("x_hi_ready"), sem("x_lo_ready")
        qk_ready, hi_ready, lo_ready = sem("qk_ready"), sem("hi_ready"), sem("lo_ready")
        v_ready, vs_ready, stored = sem("v_ready"), sem("vs_ready"), sem("stored", 2)
        STORES = 4 + 1
        LOADS = K0 * 6
        SPREAD = {1: (0, 1), 2: (2, 3)}
        block = ctx.enter_context(nc.Block())

        def product(e, out, lhs, rhs, c):
            (l_hi, l_lo), (r_hi, r_lo) = lhs, rhs
            e.matmul(out, l_hi, r_hi, start=(c == 0), stop=False)
            e.matmul(out, l_hi, r_lo, start=False, stop=False)
            return e.matmul(out, l_lo, r_hi, start=False, stop=(c == C - 1))

        @block.sync
        def _(e):
            e.dma_start(picks[:], chosen.rearrange("(o n) -> o n", o=1)).then_inc(picks_in, 16)
            e.wait_ge(picks_in, 16)

            def weights(b, ranks):
                wait(e, w_lo_ready, b * 3)
                wait(e, bias_ready, b * 2)
                for k in ranks:
                    h = e.value_load(picks[0:1, bass.ds(b * K0 + k, 1)], min_val=0, max_val=H0 - 1)
                    for n, v in enumerate((Wq, Wk, Wv)):
                        e.dma_start(stage[:, n, :, k * DH0:(k + 1) * DH0],
                                    at_step(v.rearrange("(c p) (h d) -> h p c d", p=P, d=DH0), h)).then_inc(staged, 16)
                    half = slice(k % 2 * DH0, k % 2 * DH0 + DH0)
                    for o, v in ((0, bq), (2, bk)):
                        e.dma_start(stage_bias[half, o + k // 2:o + k // 2 + 1],
                                    at_step(v.rearrange("(h d o) -> h d o", d=DH0, o=1), h)).then_inc(staged, 16)
                    e.dma_start(stage_bias_v[:, k * DH0:(k + 1) * DH0],
                                at_step(bv.rearrange("(h d) -> h d", d=DH0), h).partition_broadcast(P)).then_inc(staged, 16)

            def body(at):
                cur = at(0)
                if cur is not None:
                    s = cur
                    if s.q in SPREAD and not (isinstance(s.b, int) and s.b == B - 1):
                        weights(s.b + 1, SPREAD[s.q])
                    for ready, tile, view in ((hi_ready, hi, hi_v), (lo_ready, lo, lo_v)):
                        e.wait_ge(ready, (s.t + 1) * 4)
                        for r in range(2):
                            e.dma_start(at_step(view, s.b)[s.q, r], tile[:, s.slot, 2 * r:2 * r + 2].bitcast(F32)).then_inc(stored[s.slot], 16)
                    e.wait_ge(vs_ready, s.t + 1)
                    e.dma_start(at_step(v0_v, s.b)[s.q], vs[:, s.slot]).then_inc(stored[s.slot], 16)

            weights(0, range(K0))
            pipelined(e, NBLK, 4, body)
            for slot in range(2):
                e.wait_ge(stored[slot], 16 * STORES * NBLK // 2)

        @block.tensor
        def _(e):
            def body(at):
                s = at(0)
                if s is None:
                    return
                e.wait_ge(x_lo_ready, s.t + 1)
                e.wait_ge(x_hi_ready, s.t + 1)
                for o in range(4):
                    if s.q == 0 and o % 2 == 0:
                        e.wait_ge(w_lo_ready, s.b * 3 + o // 2 + 1)
                    wait(e, lo_ready, (s.t - 1) * 4 + o + 1)
                    for c in range(C):
                        w = [part[:, o // 2, c, o % 2 * P:(o % 2 + 1) * P] for part in (w_hi, w_lo)]
                        mm = product(e, qk_ps[:, o], w, [part[:, s.slot, c] for part in (x_hi, x_lo)], c)
                    mm.then_inc(qk_ready, 1)
                if s.q == 0:
                    e.wait_ge(w_lo_ready, s.b * 3 + 3)
                wait(e, vs_ready, s.t)
                for j in range(S):
                    for c in range(C):
                        mm = product(e, v_ps[:, j], [part[:, s.slot, c, j * P:(j + 1) * P] for part in (x_hi, x_lo)],
                                     [part[:, 2, c] for part in (w_hi, w_lo)], c)
                mm.then_inc(v_ready, 1)

            pipelined(e, NBLK, 4, body)

        @block.scalar
        def _(e):
            def body(at):
                nxt, cur = at(1), at(0)
                if cur is not None and cur.q == 0:
                    e.wait_ge(staged, (cur.b + 1) * 16 * LOADS)
                    wait(e, v_ready, cur.t)
                    for n in range(3):
                        e.activation(w_hi[:, n], stage[:, n], ACT.Copy).then_inc(w_hi_ready, 1)
                if nxt is not None:
                    wait(e, v_ready, nxt.t - 1)
                    hold(e, passed)
                    e.activation(x_hi[:, nxt.slot], tokens_of(xnT, nxt.t), ACT.Copy).then_inc(x_hi_ready, 1)
                if cur is not None:
                    s = cur
                    e.wait_ge(bias_ready, (s.b + 1) * 2)
                    wait(e, stored[s.slot], s.turn * 16 * STORES)
                    for o in range(4):
                        e.wait_ge(qk_ready, s.t * 4 + o + 1)
                        e.activation(hi[:, s.slot, o], qk_ps[:, o], ACT.Identity, bias=bias[:, o:o + 1]).then_inc(hi_ready, 1)

            pipelined(e, NBLK, 4, body)

        @block.vector
        def _(e):
            def body(at):
                nxt, cur = at(1), at(0)
                if cur is not None and cur.q == 0:
                    wait(e, v_ready, cur.t)
                    for n in range(3):
                        e.wait_ge(w_hi_ready, cur.b * 3 + n + 1)
                        e.tensor_tensor(w_lo[:, n], stage[:, n], w_hi[:, n].bitcast(F32), ALU.subtract).then_inc(w_lo_ready, 1)
                    wait(e, hi_ready, cur.t * 4)
                    wait(e, lo_ready, cur.t * 4)
                    e.tensor_copy(bias[:], stage_bias[:]).then_inc(bias_ready, 1)
                    wait(e, vs_ready, cur.t)
                    e.tensor_copy(bias_v[:], stage_bias_v[:]).then_inc(bias_ready, 1)
                if nxt is not None:
                    wait(e, v_ready, nxt.t - 1)
                    e.wait_ge(x_hi_ready, nxt.t + 1)
                    e.tensor_tensor(x_lo[:, nxt.slot], tokens_of(xnT, nxt.t), x_hi[:, nxt.slot].bitcast(F32),
                                    ALU.subtract).then_inc(x_lo_ready, 1)
                if cur is not None:
                    s = cur
                    e.wait_ge(bias_ready, (s.b + 1) * 2)
                    wait(e, stored[s.slot], s.turn * 16 * STORES)
                    for o in range(4):
                        e.wait_ge(hi_ready, s.t * 4 + o + 1)
                        e.scalar_tensor_tensor(out=lo[:, s.slot, o], in0=qk_ps[:, o], scalar=bias[:, o:o + 1],
                                               in1=hi[:, s.slot, o].bitcast(F32), op0=ALU.add, op1=ALU.subtract).then_inc(lo_ready, 1)
                    e.wait_ge(v_ready, s.t + 1)
                    e.tensor_tensor(vs[:, s.slot], v_ps[:], bias_v[:].unsqueeze(1).broadcast_to([P, S, K0 * DH0]),
                                    ALU.add).then_inc(vs_ready, 1)

            pipelined(e, NBLK, 4, body)


def attend0(nc, qk_hi, qk_lo, v0, gates, o0, ident, fold, passed):
    units = B * K0
    n_blocks = units * QB
    RA = DH0 + DH0 // 2
    RING = 8
    BANKS, CBANKS = 3, 3
    hi_v, lo_v = (a.rearrange("r u d n -> u r d n") for a in (qk_hi, qk_lo))
    v0_v = v0.rearrange("b p t (k d) -> b k p t d", k=K0)
    o0_v = o0.rearrange("(b q s p) (k d) -> b k q p s d", b=B, p=P, s=S, k=K0)
    by_vector = [x for x in range(KT) if x % 3 == 2]
    by_pool = [x for x in range(KT) if x % 3 != 2]
    NV, NP = len(by_vector) - 1, len(by_pool) - 1

    def additions(tiles, x):
        return max(tiles.index(x), 1)

    with ExitStack() as ctx:
        sb, pb, sem = names(nc, ctx, "attend0")
        qa, ka = sb("qa", [RA, 2, T], F32R), sb("ka", [RA, 2, T], F32R)
        qb, kb = sb("qb", [RA + 1, 2, T], F32R), sb("kb", [RA + 1, 2, T], F32R)
        v = sb("v", [P, 2, KT, DH0])
        gate, scale = sb("gate", [P, units]), sb("scale", [P, units])
        gate_u, scale_u = sb("gate_u", [P, 2]), sb("scale_u", [P, 2])
        ones = sb("ones", [P, 1])
        probs = sb("probs", [P, RING, BLOCK])
        sum_v, sum_p, sums = sb("sum_v", [P, BLOCK]), sb("sum_p", [P, BLOCK]), sb("sums", [P, 2, BLOCK])
        part = sb("part", [P, S, QB])
        peak, row = sb("peak", [P, S]), sb("row", [S, 2, P], F32R)
        u = sb("u", [P, BLOCK])
        inv, factor = sb("inv", [P, S]), sb("factor", [P, S])
        out = sb("out", [P, 2, S, DH0])
        score_ps = pb("score_ps", [P, BANKS, BLOCK])
        chunk_ps = pb("chunk_ps", [P, CBANKS, BLOCK])
        pv_ps, fold_ps = (pb(n, [P, BLOCK]) for n in ("pv_ps", "fold_ps"))
        row_ps = fold_ps[0:S, BLOCK - P:]

        gates_in, consts, scaled, staged = sem("gates_in"), sem("consts"), sem("scaled"), sem("staged")
        unit_in = sem("unit_in", 2)
        chunk_ready, chunk_read = sem("chunk_ready"), sem("chunk_read")
        peaked, peak_turned, row_ready, row_in = sem("peaked"), sem("peak_turned"), sem("row_ready"), sem("row_in", 2)
        scores_ready, exp_done, pv_done = sem("scores_ready"), sem("exp_done"), sem("pv_done")
        added_v, added_p, summed = sem("added_v"), sem("added_p"), sem("summed")
        u_ready, folded, inverted, out_ready, out_stored = (sem("u_ready"), sem("folded"), sem("inverted"),
                                                            sem("out_ready"), sem("out_stored", 2))
        LOADS = 9
        block = ctx.enter_context(nc.Block())

        @block.sync
        def _(e):
            def load(s):
                wait(e, pv_done, (s.b - 1) * QB * KT)
                half, i = DH0 // 2, s.side
                h, l = at_step(hi_v, s.b), at_step(lo_v, s.b)
                for dst, src in ((ka[0:DH0, i], h[1]), (ka[DH0:RA, i], h[1, 0:half]), (qa[0:DH0, i], h[0]),
                                 (qa[DH0:RA, i], l[0, 0:half]), (qb[0:half, i], l[0, half:DH0]), (qb[half:RA, i], h[0]),
                                 (kb[0:half, i], h[1, half:DH0]), (kb[half:RA, i], l[1])):
                    e.dma_start(dst.bitcast(F32), src).then_inc(unit_in[i], 16)
                e.dma_start(v[:, i], at_step(at_step(v0_v, s.b // K0), s.b % K0)).then_inc(unit_in[i], 16)

            def body(at):
                first, mid, prev = at(4), at(1), at(-1)
                if first is not None and first.q == 0:
                    load(first)
                if mid is not None:
                    e.wait_ge(row_ready, mid.t + 1)
                    e.dma_start(qb[RA:RA + 1, mid.side, mid.q * BLOCK:(mid.q + 1) * BLOCK].bitcast(F32)
                                .rearrange("o (s p) -> o s p", s=S), row[:, mid.slot].bitcast(F32)).then_inc(row_in[mid.slot], 16)
                if prev is not None:
                    e.wait_ge(out_ready, prev.t + 1)
                    hold(e, passed)
                    e.dma_start(at_step(at_step(o0_v, prev.b // K0), prev.b % K0)[prev.q], out[:, prev.slot]).then_inc(out_stored[prev.slot], 16)

            e.dma_start(gate[:], gates.partition_broadcast(P)).then_inc(gates_in, 16)
            pipelined(e, n_blocks, 2 * QB, body, ahead=4)
            for slot in range(2):
                e.wait_ge(out_stored[slot], 16 * n_blocks // 2)

        before = [x - BANKS if x >= BANKS else max(y for y in range(KT) if y % BANKS == x) - KT for x in range(KT)]
        chunk_before = [x - CBANKS if x >= CBANKS else max(y for y in range(KT) if y % CBANKS == x) - KT for x in range(KT)]
        VALUES_AT = {4: (0, 2), 8: (2, 6), 12: (6, 10), KT - 1: (10, KT - 2)}
        @block.tensor
        def _(e):
            e.wait_ge(consts, 2)

            def chunk(s, x):
                j, kc = x // QB, x % QB
                if x == 0:
                    e.wait_ge(unit_in[s.side], (s.uses + 1) * 16 * LOADS)
                wait(e, chunk_read, s.t * KT + chunk_before[x] + 1)
                e.matmul(chunk_ps[:, x % CBANKS], qa[:, s.side, s.q * BLOCK + j * P:s.q * BLOCK + (j + 1) * P],
                         ka[:, s.side, kc * BLOCK:(kc + 1) * BLOCK], start=True, stop=True).then_inc(chunk_ready, 1)

            def pv(s, x):
                if x == 0:
                    wait(e, u_ready, s.t)
                e.wait_ge(exp_done, s.t * KT + x + 1)
                half = slice(x % 2 * DH0, x % 2 * DH0 + DH0)
                e.matmul(pv_ps[half, :], v[:, s.side, x], probs[:, x % RING], start=(x < 2), stop=(x >= KT - 2))\
                    .then_inc(pv_done, 1)

            def finish(s, j, rows):
                if j == 0:
                    e.wait_ge(u_ready, s.t + 1)
                    e.wait_ge(summed, s.t + 1)
                    wait(e, out_ready, s.t)
                    e.wait_ge(row_ready, rows)
                e.matmul(fold_ps[:, j * DH0:(j + 1) * DH0], u[:, j * P:(j + 1) * P], fold, start=True, stop=True)
                e.matmul(fold_ps[:, S * DH0 + j:S * DH0 + j + 1], sums[:, s.slot, j * P:(j + 1) * P], ones[:],
                         start=True, stop=True).then_inc(folded, 1)

            def body(at):
                far, mid, cur, prev = at(2), at(1), at(0), at(-1)
                for x in range(KT):
                    if cur is not None:
                        if x == 0:
                            e.wait_ge(row_in[cur.slot], (cur.turn + 1) * 16)
                        wait(e, exp_done, cur.t * KT + before[x] + 1)
                        for half, (k_, q_) in enumerate(((ka, qa), (kb, qb))):
                            mm = e.matmul(score_ps[:, x % BANKS], k_[:, cur.side, x * P:(x + 1) * P],
                                          q_[:, cur.side, cur.q * BLOCK:(cur.q + 1) * BLOCK], start=(half == 0), stop=(half == 1))
                        mm.then_inc(scores_ready, 1)
                    if far is not None:
                        chunk(far, x)
                    if mid is not None and x == 1:
                        e.wait_ge(peaked, mid.t + 1)
                        wait(e, row_ready, mid.t)
                        wait(e, out_ready, mid.t - 2)
                        e.transpose(row_ps, peak[:], ident).then_inc(peak_turned, 1)
                    if cur is not None and x in VALUES_AT:
                        for y in range(*VALUES_AT[x]):
                            pv(cur, y)
                    if prev is not None and 4 <= x < 4 + S:
                        finish(prev, x - 4, n_blocks if mid is None else mid.t + 1)
                if cur is not None:
                    pv(cur, KT - 2)
                    pv(cur, KT - 1)

            pipelined(e, n_blocks, 2 * QB, body, ahead=2)

        @block.scalar
        def _(e):
            def body(at):
                s = at(0)
                if s is None:
                    return
                if s.q == 0:
                    e.wait_ge(staged, (s.b + 1) * 2)
                for x in range(KT):
                    e.wait_ge(scores_ready, s.t * KT + x + 1)
                    old, back = (s.t, x - RING) if x >= RING else (s.t - 1, x - RING + KT)
                    wait(e, pv_done, s.t * KT + x - RING + 1)
                    tiles, sem_, n = (by_vector, added_v, NV) if back in by_vector else (by_pool, added_p, NP)
                    wait(e, sem_, old * n + additions(tiles, back))
                    e.activation(probs[:, x % RING], score_ps[:, x % BANKS], ACT.Exp,
                                 scale=scale_u[:, s.side:s.side + 1]).then_inc(exp_done, 1)
                e.wait_ge(pv_done, (s.t + 1) * KT)
                wait(e, folded, s.t * S)
                e.activation(u[:], pv_ps[:], ACT.Copy).then_inc(u_ready, 1)

            pipelined(e, n_blocks, 2 * QB, body, ahead=0, behind=1)

        @block.gpsimd
        def _(e):
            def body(at):
                s = at(0)
                if s is None:
                    return
                for m in range(1, len(by_pool)):
                    x = by_pool[m]
                    e.wait_ge(exp_done, s.t * KT + x + 1)
                    if m == 1:
                        wait(e, summed, s.t)
                        a = probs[:, by_pool[0] % RING]
                    else:
                        e.wait_ge(added_p, s.t * NP + m - 1)
                        a = sum_p[:]
                    e.tensor_tensor(sum_p[:], a, probs[:, x % RING], ALU.add).then_inc(added_p, 1)

            pipelined(e, n_blocks, 2 * QB, body, ahead=0, behind=1)

        @block.vector
        def _(e):
            e.memset(ones[:], 1.0).then_inc(consts, 1)
            e.memset(kb[RA:RA + 1].bitcast(F32), 1.0).then_inc(consts, 1)
            e.wait_ge(gates_in, 16)
            e.tensor_scalar(scale[:], gate[:], DH0 ** -0.5, None, ALU.mult).then_inc(scaled, 1)
            e.wait_ge(scaled, 1)
            e.tensor_tensor(scale[:], scale[:], gate[:], ALU.mult).then_inc(scaled, 1)
            e.wait_ge(scaled, 2)

            def read(s, x):
                e.wait_ge(chunk_ready, s.t * KT + x + 1)
                if x == 0:
                    wait(e, peaked, s.t)
                e.tensor_reduce(part[:, x // QB, x % QB:x % QB + 1], chunk_ps[:, x % CBANKS], AX.X, ALU.max).then_inc(chunk_read, 1)

            def add(s, x):
                m = by_vector.index(x)
                if m == 0:
                    return
                e.wait_ge(exp_done, s.t * KT + x + 1)
                if m == 1:
                    wait(e, summed, s.t)
                    a = probs[:, by_vector[0] % RING]
                else:
                    e.wait_ge(added_v, s.t * NV + m - 1)
                    a = sum_v[:]
                e.tensor_tensor(sum_v[:], a, probs[:, x % RING], ALU.add).then_inc(added_v, 1)

            def total(s):
                e.wait_ge(added_p, (s.t + 1) * NP)
                e.wait_ge(added_v, (s.t + 1) * NV)
                wait(e, folded, (s.t - 1) * S)
                e.tensor_tensor(sums[:, s.slot], sum_v[:], sum_p[:], ALU.add).then_inc(summed, 1)

            def normalise(s):
                e.wait_ge(folded, (s.t + 1) * S)
                e.reciprocal(inv[:], fold_ps[:, S * DH0:S * DH0 + S]).then_inc(inverted, 1)
                e.wait_ge(inverted, s.t * 2 + 1)
                e.tensor_scalar(factor[:], inv[:], gate_u[:, s.side:s.side + 1], None, ALU.mult).then_inc(inverted, 1)
                e.wait_ge(inverted, s.t * 2 + 2)
                wait(e, out_stored[s.slot], s.turn * 16)
                e.tensor_tensor(out[:, s.slot], fold_ps[:, 0:S * DH0].rearrange("p (s d) -> p s d", s=S),
                                factor[:].unsqueeze(2).broadcast_to([P, S, DH0]), ALU.mult).then_inc(out_ready, 1)

            def body(at):
                far, mid, cur, prev = at(2), at(1), at(0), at(-1)
                if mid is not None and mid.q == 0:
                    wait(e, exp_done, (mid.b - 1) * QB * KT)
                    e.tensor_copy(scale_u[:, mid.side:mid.side + 1], scale[:, bass.ds(mid.b, 1)]).then_inc(staged, 1)
                    e.tensor_copy(gate_u[:, mid.side:mid.side + 1], gate[:, bass.ds(mid.b, 1)]).then_inc(staged, 1)
                for x in range(KT):
                    if far is not None:
                        read(far, x)
                    if mid is not None and x == 2:
                        e.wait_ge(peak_turned, mid.t + 1)
                        wait(e, row_in[mid.slot], mid.turn * 16)
                        e.tensor_copy(row[:, mid.slot], row_ps).then_inc(row_ready, 1)
                    if cur is not None and x - 3 in by_vector:
                        add(cur, x - 3)
                    if prev is not None and x == 1:
                        total(prev)
                    if prev is not None and x == 9:
                        normalise(prev)
                if far is not None:
                    e.wait_ge(chunk_read, (far.t + 1) * KT)
                    wait(e, peak_turned, far.t)
                    e.tensor_reduce(peak[:], part[:], AX.X, ALU.max, negate=True).then_inc(peaked, 1)
                if cur is not None:
                    for x in (KT - 3, KT - 2, KT - 1):
                        if x in by_vector:
                            add(cur, x)

            pipelined(e, n_blocks, 2 * QB, body, ahead=2)


def between(nc, x, o0, yT, W_o0, b_o0, Wq, Wk, Wv, bq, bk, bv, b_o1, W_r, W_k, W_v, mu_r, mu_k, ident, parts1, v1, base, passed):
    x_v = x.rearrange("b (q s p) d -> (b q) p s d", p=P, s=S)
    o0_v = o0.rearrange("(t s p) e -> t p s e", p=P, s=S)
    yT_v = yT.rearrange("(c p) (t n) -> t p c n", p=P, n=BLOCK)
    parts_v = parts1.rearrange("a r b (o p) (q n) -> b q a r p o n", p=P, n=BLOCK)
    v1_v = v1.rearrange("(b g) p (q s) e -> b q g p s e", b=B, s=S)
    base_v = base.rearrange("(t s p) d -> t p s d", p=P, s=S)
    HV = 2 * DH1
    with ExitStack() as ctx:
        sb, pb, sem = names(nc, ctx, "between")
        wo = sb("wo", [P, C, D])
        whole, w_hi, w_lo = sb("whole", [P, 3, C, D]), sb("w_hi", [P, 3, C, D], F32R), sb("w_lo", [P, 3, C, D], F32R)
        natural = sb("natural", [P, 3, C, D])
        turned_w = sb("turned_w", [P, 3, C, D])
        bias = sb("bias", [P, 4])
        mu, nu = sb("mu", [P, 2, C]), sb("nu", [P, 2, C])
        bo0, bo1, bias_v = sb("bo0", [P, D]), sb("bo1", [P, D]), sb("bias_v", [P, D])
        eps = sb("eps", [P, 1])
        xin, oin, yin = sb("xin", [P, 2, S, D]), sb("oin", [P, 2, S, D]), sb("yin", [P, 2, C, BLOCK])
        ot = sb("ot", [P, C, BLOCK])
        x_bias, x2, x2_bias = sb("x_bias", [P, S, D]), sb("x2", [P, S, D]), sb("x2_bias", [P, 2, S, D])
        st, mv = sb("st", [P, S, 6]), sb("mv", [P, S, 2])
        dev, inv = sb("dev", [P, S]), sb("inv", [P, S])
        xn = sb("xn", [P, S, D])
        xs = sb("xs", [P, 2, C, BLOCK + 1])
        xs_hi, xs_lo = sb("xs_hi", [P, C, BLOCK], F32R), sb("xs_lo", [P, C, BLOCK], F32R)
        share = sb("share", [P, 2, C, BLOCK])
        mix = sb("mix", [P, 2, 2, C, BLOCK])
        parts = sb("parts", [P, 2, 3, 4, BLOCK], BF16)
        left = sb("left", [P, 4, BLOCK])
        relu, act = sb("relu", [P, C, BLOCK]), sb("act", [P, C, BLOCK])
        tanh_r = sb("tanh_r", [P, S, D])
        ff, total = sb("ff", [P, S, D]), sb("total", [P, S, D])
        vs = sb("vs", [P, 2, S, H1, HV])
        turn_ps, x2_ps = pb("turn_ps", [P, C, BLOCK]), pb("x2_ps", [P, S, D])
        even_ps, odd_ps = pb("even_ps", [P, 2, BLOCK]), pb("odd_ps", [P, 2, BLOCK])

        weights_in, prepared, w_turned, w_ready = sem("weights_in"), sem("prepared"), sem("w_turned"), sem("w_ready")
        x_in, o_in, y_in = sem("x_in", 2), sem("o_in", 2), sem("y_in", 2)
        w_hi_ready, w_lo_ready = sem("w_hi_ready"), sem("w_lo_ready")
        o_turned, ot_ready, x2_summed = sem("o_turned"), sem("ot_ready"), sem("x2_summed")
        xs_hi_ready, xs_lo_ready = sem("xs_hi_ready"), sem("xs_lo_ready")
        x_biased, x2_ready, x2_biased = sem("x_biased"), sem("x2_ready"), sem("x2_biased")
        stats, deviation, inverse, normed = sem("stats"), sem("deviation"), sem("inverse"), sem("normed")
        xn_turned, xs_ready, carried = sem("xn_turned"), sem("xs_ready"), sem("carried")
        shared, mixed = sem("shared"), sem("mixed")
        q_ready, k_ready, kf_ready, v_ready, r_ready, vf_ready = (sem(n) for n in (
            "q_ready", "k_ready", "kf_ready", "v_ready", "r_ready", "vf_ready"))
        part_h, rest_h, part_m, part_l = sem("part_h"), sem("rest_h"), sem("part_m"), sem("part_l")
        rectified, squared, squashed = sem("rectified"), sem("squared"), sem("squashed")
        vs_ready, gated, total_ready = sem("vs_ready"), sem("gated"), sem("total_ready")
        parts_out, vs_out, total_out = sem("parts_out", 2), sem("vs_out", 2), sem("total_out")
        WEIGHTS = 4 + 3 + 2 + 2 + 3
        block = ctx.enter_context(nc.Block())

        @block.sync
        def _(e):
            for w, v in ((wo[:], W_o0), (whole[:, 0], Wq), (whole[:, 1], Wk), (whole[:, 2], Wv)):
                e.dma_start(w, v.rearrange("(c p) h -> p c h", p=P)).then_inc(weights_in, 16)
            for n, v in enumerate((W_r, W_k, W_v)):
                e.dma_start(natural[:, n], v.rearrange("(o p) c -> p o c", p=P)).then_inc(weights_in, 16)
            for n, v in enumerate((bq, bk)):
                e.dma_start(bias[:, 2 * n:2 * n + 2], v.rearrange("(c p) -> p c", p=P), allow_slow_non_contiguous=True)\
                    .then_inc(weights_in, 16)
            for n, v in enumerate((mu_r, mu_k)):
                e.dma_start(mu[:, n], v.rearrange("(c p) -> p c", p=P), allow_slow_non_contiguous=True).then_inc(weights_in, 16)
            for w, v in ((bo0, b_o0), (bo1, b_o1), (bias_v, bv)):
                e.dma_start(w[:], v.partition_broadcast(P)).then_inc(weights_in, 16)

            def body(at):
                nxt, cur = at(2), at(0)
                if nxt is not None:
                    s = nxt
                    wait(e, x_biased, s.t - 1)
                    e.dma_start(xin[:, s.slot], at_step(x_v, s.t)).then_inc(x_in[s.slot], 16)
                    wait(e, o_turned, s.t - 1)
                    e.dma_start(oin[:, s.slot], at_step(o0_v, s.t)).then_inc(o_in[s.slot], 16)
                    wait(e, x2_summed, s.t - 1)
                    e.dma_start(yin[:, s.slot], at_step(yT_v, s.t)).then_inc(y_in[s.slot], 16)
                if cur is not None:
                    s = cur
                    e.wait_ge(part_m, (s.t + 1) * 4)
                    e.wait_ge(part_l, (s.t + 1) * 4)
                    for a in range(3):
                        for r in range(2):
                            e.dma_start(at_step(parts_v, s.b)[s.q, a, r], parts[:, s.slot, a, 2 * r:2 * r + 2])\
                                .then_inc(parts_out[s.slot], 16)
                    e.wait_ge(vs_ready, s.t + 1)
                    for g in range(H1 // G1):
                        e.dma_start(at_step(v1_v, s.b)[s.q, g],
                                    vs[:, s.slot, :, g * G1:(g + 1) * G1].rearrange("p s h e -> p s (h e)")).then_inc(vs_out[s.slot], 16)
                    e.wait_ge(total_ready, s.t + 1)
                    e.dma_start(at_step(base_v, s.t), total[:]).then_inc(total_out, 16)

            pipelined(e, NBLK, 4, body, ahead=2)
            for slot in range(2):
                e.wait_ge(parts_out[slot], 16 * 6 * NBLK // 2)
                e.wait_ge(vs_out[slot], 16 * (H1 // G1) * NBLK // 2)
            e.wait_ge(total_out, 16 * NBLK)

        @block.tensor
        def _(e):
            e.wait_ge(weights_in, 16 * WEIGHTS)
            for n in range(3):
                if n > 0:
                    e.wait_ge(w_ready, n)
                for c in range(C):
                    for o in range(C):
                        mm = e.transpose(turn_ps[:, c, o * P:(o + 1) * P], natural[:, n, o, c * P:(c + 1) * P], ident)
                mm.then_inc(w_turned, 1)
            e.wait_ge(w_ready, 3)
            e.wait_ge(w_lo_ready, 3)

            def product(out, lhs, rhs, first, last):
                (l_hi, l_lo), (r_hi, r_lo) = lhs, rhs
                e.matmul(out, l_hi, r_hi, start=first, stop=False, skip_group_check=True)
                e.matmul(out, l_lo, r_hi, start=False, stop=False, skip_group_check=True)
                return e.matmul(out, l_hi, r_lo, start=False, stop=last, skip_group_check=True)

            def columns_by_parts(out, n, ready):
                for o in range(C):
                    for c in range(C):
                        mm = product(out[:, o], [w[:, n, c, o * P:(o + 1) * P] for w in (w_hi, w_lo)],
                                     [x_[:, c] for x_ in (xs_hi, xs_lo)], c == 0, c == C - 1)
                    mm.then_inc(ready, 1)

            def tokens_by_parts(out, n, ready):
                out = out[:].rearrange("p a (b d) -> p (a b) d", d=D)
                for j in range(S):
                    for c in range(C):
                        mm = product(out[:, j], [x_[:, c, j * P:(j + 1) * P] for x_ in (xs_hi, xs_lo)],
                                     [w[:, n, c] for w in (w_hi, w_lo)], c == 0, c == C - 1)
                mm.then_inc(ready, 1)

            def columns(out, w, rhs, ready):
                for o in range(C):
                    for c in range(C):
                        mm = e.matmul(out[:, o], w[:, c, o * P:(o + 1) * P], rhs[:, c], start=(c == 0), stop=(c == C - 1))
                    mm.then_inc(ready, 1)

            def tokens(out, lhs, w, ready):
                out = out[:].rearrange("p a (b d) -> p (a b) d", d=D)
                for j in range(S):
                    for c in range(C):
                        mm = e.matmul(out[:, j], lhs[:, c, j * P:(j + 1) * P], w[:, c], start=(c == 0), stop=(c == C - 1))
                mm.then_inc(ready, 1)

            def body(at):
                nxt, cur = at(1), at(0)
                if nxt is not None:
                    s = nxt
                    e.wait_ge(o_in[s.slot], (s.turn + 1) * 16)
                    wait(e, xs_ready, s.t * C)
                    wait(e, xs_hi_ready, s.t * C)
                    for j in range(S):
                        for c in range(C):
                            mm = e.transpose(turn_ps[:, c, j * P:(j + 1) * P], oin[:, s.slot, j, c * P:(c + 1) * P], ident)
                    mm.then_inc(o_turned, 1)
                if cur is not None:
                    s, t = cur, cur.t
                    e.wait_ge(xs_hi_ready, (t + 1) * C)
                    e.wait_ge(xs_lo_ready, (t + 1) * C)
                    wait(e, squashed, t)
                    columns_by_parts(even_ps, 0, q_ready)
                if nxt is not None:
                    s = nxt
                    e.wait_ge(ot_ready, (s.t + 1) * C)
                    e.wait_ge(y_in[s.slot], (s.turn + 1) * 16)
                    wait(e, x2_ready, s.t)
                    for j in range(S):
                        for c in range(C):
                            e.matmul(x2_ps[:, j], ot[:, c, j * P:(j + 1) * P], wo[:, c], start=(c == 0), stop=False,
                                     skip_group_check=True)
                        for c in range(C):
                            mm = e.matmul(x2_ps[:, j, c * P:(c + 1) * P], yin[:, s.slot, c, j * P:(j + 1) * P], ident,
                                          start=False, stop=(c == C - 1), skip_group_check=True)
                    mm.then_inc(x2_summed, 1)
                if cur is not None:
                    s, t = cur, cur.t
                    wait(e, gated, t)
                    columns_by_parts(odd_ps, 1, k_ready)
                    e.wait_ge(rest_h, t * 4 + 2)
                    e.wait_ge(mixed, (t + 1) * 2 * C)
                    columns(even_ps, turned_w[:, 1], mix[:, s.slot, 1], kf_ready)
                    e.wait_ge(rest_h, t * 4 + 4)
                    tokens_by_parts(odd_ps, 2, v_ready)
                    e.wait_ge(rectified, t + 1)
                    tokens(even_ps, mix[:, s.slot, 0], turned_w[:, 0], r_ready)
                if nxt is not None:
                    s = nxt
                    e.wait_ge(normed, (s.t + 1) * S)
                    for j in range(S):
                        for c in range(C):
                            mm = e.transpose(turn_ps[:, c, j * P:(j + 1) * P], xn[:, j, c * P:(c + 1) * P], ident)
                    mm.then_inc(xn_turned, 1)
                if cur is not None:
                    e.wait_ge(squared, cur.t + 1)
                    e.wait_ge(vs_ready, cur.t + 1)
                    tokens(odd_ps, act, turned_w[:, 2], vf_ready)

            pipelined(e, NBLK, 4, body)

        @block.scalar
        def _(e):
            for n in range(3):
                e.wait_ge(w_turned, n + 1)
                e.activation(turned_w[:, n], turn_ps[:, :, 0:D], ACT.Copy).then_inc(w_ready, 1)
            for n in range(3):
                e.activation(w_hi[:, n], whole[:, n], ACT.Copy).then_inc(w_hi_ready, 1)
            e.wait_ge(prepared, 3)

            def body(at):
                nxt, cur = at(1), at(0)
                if nxt is not None:
                    e.wait_ge(o_turned, nxt.t + 1)
                    wait(e, x2_summed, nxt.t)
                    for c in range(C):
                        e.activation(ot[:, c], turn_ps[:, c], ACT.Copy).then_inc(ot_ready, 1)
                if cur is not None:
                    s, t = cur, cur.t
                    wait(e, parts_out[s.slot], s.turn * 16 * 6)
                    for o in range(4):
                        if o < 2:
                            e.wait_ge(q_ready, t * 2 + o + 1)
                        else:
                            e.wait_ge(k_ready, t * 2 + o - 1)
                        src = (even_ps, odd_ps)[o // 2][:, o % 2]
                        e.activation(parts[:, s.slot, 0, o], src, ACT.Identity, bias=bias[:, o:o + 1]).then_inc(part_h, 1)
                    e.wait_ge(kf_ready, (t + 1) * 2)
                    wait(e, squared, t)
                    e.activation(relu[:], even_ps[:], ACT.Relu).then_inc(rectified, 1)
                if nxt is not None:
                    e.wait_ge(stats, (nxt.t + 1) * 2 * S)
                    e.activation(dev[:], mv[:, :, 1], ACT.Sqrt, bias=eps[:, 0:1]).then_inc(deviation, 1)
                if cur is not None:
                    e.wait_ge(r_ready, cur.t + 1)
                    wait(e, gated, cur.t)
                    e.activation(tanh_r[:], even_ps[:].rearrange("p a (b d) -> p (a b) d", d=D), ACT.Tanh, scale=0.5)\
                        .then_inc(squashed, 1)
                if nxt is not None:
                    s = nxt
                    e.wait_ge(xn_turned, s.t + 1)
                    wait(e, v_ready, s.t)
                    wait(e, mixed, (s.t - 1) * 2 * C)
                    wait(e, carried, s.t)
                    for c in range(C):
                        e.activation(xs[:, s.slot, c, 1:], turn_ps[:, c], ACT.Copy).then_inc(xs_ready, 1)
                        e.activation(xs_hi[:, c], turn_ps[:, c], ACT.Copy).then_inc(xs_hi_ready, 1)

            pipelined(e, NBLK, 4, body)

        @block.gpsimd
        def _(e):
            e.memset(eps[:], EPS).then_inc(prepared, 1)
            e.memset(vs[:], 1.0).then_inc(prepared, 1)
            e.wait_ge(weights_in, 16 * WEIGHTS)

            def body(at):
                nxt, cur = at(1), at(0)
                if nxt is not None:
                    s = nxt
                    e.wait_ge(x_in[s.slot], (s.turn + 1) * 16)
                    wait(e, x2_ready, s.t)
                    e.tensor_tensor(x_bias[:], xin[:, s.slot], bo0[:].unsqueeze(1).broadcast_to([P, S, D]), ALU.add)\
                        .then_inc(x_biased, 1)
                if cur is not None:
                    s, t = cur, cur.t
                    wait(e, parts_out[s.slot], s.turn * 16 * 6)
                    for o in range(4):
                        e.wait_ge(part_m, t * 4 + o + 1)
                        e.tensor_tensor(parts[:, s.slot, 2, o], left[:, o], parts[:, s.slot, 1, o], ALU.subtract).then_inc(part_l, 1)
                    e.wait_ge(rectified, t + 1)
                    wait(e, vf_ready, t)
                    e.tensor_tensor(act[:], relu[:], relu[:], ALU.mult).then_inc(squared, 1)
                if nxt is not None:
                    s = nxt
                    e.wait_ge(x2_ready, s.t + 1)
                    wait(e, total_ready, s.t - 1)
                    e.tensor_tensor(x2_bias[:, s.slot], x2[:], bo1[:].unsqueeze(1).broadcast_to([P, S, D]), ALU.add)\
                        .then_inc(x2_biased, 1)
                    wait(e, v_ready, s.t)
                    for c in range(C):
                        e.wait_ge(xs_ready, s.t * C + c + 1)
                        e.wait_ge(xs_hi_ready, s.t * C + c + 1)
                        e.tensor_tensor(xs_lo[:, c], xs[:, s.slot, c, 1:], xs_hi[:, c].bitcast(F32), ALU.subtract).then_inc(xs_lo_ready, 1)

            pipelined(e, NBLK, 4, body)

        @block.vector
        def _(e):
            e.wait_ge(weights_in, 16 * WEIGHTS)
            e.tensor_scalar(nu[:], mu[:], -1.0, 1.0, ALU.mult, ALU.add).then_inc(prepared, 1)
            for n in range(3):
                e.wait_ge(w_hi_ready, n + 1)
                e.tensor_tensor(w_lo[:, n], whole[:, n], w_hi[:, n].bitcast(F32), ALU.subtract).then_inc(w_lo_ready, 1)
            e.wait_ge(prepared, 3)

            def split(s, o):
                t = s.t
                e.wait_ge(part_h, t * 4 + o + 1)
                wait(e, part_l, (t - 1) * 4 + o + 1)
                src = (even_ps, odd_ps)[o // 2][:, o % 2]
                e.scalar_tensor_tensor(out=left[:, o], in0=src, scalar=bias[:, o:o + 1], in1=parts[:, s.slot, 0, o],
                                       op0=ALU.add, op1=ALU.subtract).then_inc(rest_h, 1)
                e.wait_ge(rest_h, t * 4 + o + 1)
                e.tensor_copy(parts[:, s.slot, 1, o], left[:, o]).then_inc(part_m, 1)

            def body(at):
                nxt, cur = at(1), at(0)
                if cur is not None:
                    wait(e, parts_out[cur.slot], cur.turn * 16 * 6)
                    split(cur, 0)
                    split(cur, 1)
                if nxt is not None:
                    s = nxt
                    e.wait_ge(x2_summed, s.t + 1)
                    e.wait_ge(x_biased, s.t + 1)
                    wait(e, x2_biased, s.t)
                    wait(e, normed, s.t * S)
                    e.tensor_tensor(x2[:], x2_ps[:], x_bias[:], ALU.add).then_inc(x2_ready, 1)
                    e.wait_ge(x2_ready, s.t + 1)
                    for j in range(S):
                        e.bn_stats(st[:, j], x2[:, j]).then_inc(stats, 1)
                    e.wait_ge(stats, s.t * 2 * S + S)
                    hold(e, passed)
                    for j in range(S):
                        e.bn_aggr(mv[:, j], st[:, j]).then_inc(stats, 1)
                if cur is not None:
                    split(cur, 2)
                    split(cur, 3)
                    e.wait_ge(v_ready, cur.t + 1)
                    wait(e, vs_out[cur.slot], cur.turn * 16 * (H1 // G1))
                    e.tensor_tensor(vs[:, cur.slot, :, :, 0:DH1],
                                    odd_ps[:].rearrange("p a (b h d) -> p (a b) h d", b=S // 2, h=H1),
                                    bias_v[:].rearrange("p (h d) -> p h d", h=H1).unsqueeze(1).broadcast_to([P, S, H1, DH1]),
                                    ALU.add).then_inc(vs_ready, 1)
                if nxt is not None:
                    s = nxt
                    e.wait_ge(deviation, s.t + 1)
                    e.reciprocal(inv[:], dev[:]).then_inc(inverse, 1)
                    wait(e, xn_turned, s.t)
                    e.wait_ge(inverse, s.t + 1)
                    for j in range(S):
                        e.tensor_scalar(xn[:, j], x2[:, j], mv[:, j, 0:1], inv[:, j:j + 1],
                                        ALU.subtract, ALU.mult).then_inc(normed, 1)
                if cur is not None:
                    s, t = cur, cur.t
                    e.wait_ge(vf_ready, t + 1)
                    e.wait_ge(squashed, t + 1)
                    wait(e, total_ready, t)
                    e.scalar_tensor_tensor(out=ff[:], in0=tanh_r[:], scalar=1.0,
                                           in1=odd_ps[:].rearrange("p a (b d) -> p (a b) d", d=D),
                                           op0=ALU.add, op1=ALU.mult).then_inc(gated, 1)
                    e.wait_ge(gated, t + 1)
                    e.wait_ge(x2_biased, t + 1)
                    wait(e, total_out, t * 16)
                    e.scalar_tensor_tensor(out=total[:], in0=ff[:], scalar=0.5, in1=x2_bias[:, s.slot],
                                           op0=ALU.mult, op1=ALU.add).then_inc(total_ready, 1)
                if nxt is not None:
                    s = nxt
                    wait(e, mixed, (s.t - 1) * 2 * C)
                    wait(e, v_ready, s.t - 1)
                    if s.q == 0:
                        e.memset(xs[:, s.slot, :, 0:1], 0.0).then_inc(carried, 1)
                    else:
                        e.wait_ge(xs_ready, s.t * C)
                        e.tensor_copy(xs[:, s.slot, :, 0:1], xs[:, 1 - s.slot, :, BLOCK:BLOCK + 1]).then_inc(carried, 1)
                    e.wait_ge(carried, s.t + 1)
                    e.wait_ge(xs_ready, (s.t + 1) * C)
                    wait(e, r_ready, s.t - 1)
                    wait(e, mixed, s.t * 2 * C)
                    for n in range(2):
                        if n > 0:
                            e.wait_ge(mixed, s.t * 2 * C + C)
                        for c in range(C):
                            e.tensor_scalar(share[:, n, c], xs[:, s.slot, c, 0:BLOCK], nu[:, n, c:c + 1], None, ALU.mult)\
                                .then_inc(shared, 1)
                        for c in range(C):
                            e.wait_ge(shared, (s.t * 2 + n) * C + c + 1)
                            e.scalar_tensor_tensor(out=mix[:, s.slot, n, c], in0=xs[:, s.slot, c, 1:],
                                                   scalar=mu[:, n, c:c + 1], in1=share[:, n, c],
                                                   op0=ALU.mult, op1=ALU.add).then_inc(mixed, 1)

            pipelined(e, NBLK, 4, body)


def attend1(nc, parts1, v1, o1, ident, upper, passed):
    units = B * H1 // G1
    R = 6 * DH1
    Q_PARTS, K_PARTS = (0, 0, 1, 0, 2, 1), (0, 1, 0, 2, 0, 1)
    HV = 2 * DH1
    RING, BANKS, LEAD = 16, 3, 88
    CBANKS = 3
    GROUPS = [(q, kt) for q in range(QB) for kt in range(S * (q + 1))]
    NG = len(GROUPS)
    N = NG * G1
    LAST = [max(g for g in range(NG) if GROUPS[g][0] == q) for q in range(QB)]
    CHUNKS = [(q, j, h, kc) for q in range(QB) for j in range(S) for h in range(G1) for kc in range(q + 1)]
    assert len(CHUNKS) == N and NG % 2 == 0
    CHUNK_END = [(LAST[q] + 1) * G1 for q in range(QB)]

    def after_block(g, lag):
        return [(d, q) for d in (-1, 0) for q in range(QB) if LAST[q] + lag == g - d * NG]

    def after_maxima(g, lag):
        return [(d, q) for d in (0, 1) for q in range(QB) if (CHUNK_END[q] - LEAD) // G1 - 1 + lag == g - d * NG]

    def chunk_at(x):
        return (0, x + LEAD) if x + LEAD < N else (1, x + LEAD - N)

    MASKED = [sum(1 for q, kt in GROUPS[:g + 1] if kt >= S * q) * G1 for g in range(NG)]

    def same_bank_before(x, banks):
        return x - banks if x >= banks else max(y for y in range(N) if y % banks == x) - N

    before, chunk_before = ([same_bank_before(x, banks) for x in range(N)] for banks in (BANKS, CBANKS))

    def turns_before(at, g, after, lag):
        t = [at(d).t - d for d in (-1, 0, 1) if at(d) is not None][0]
        ahead = sum(1 for x in range(g) for d, _ in after(x, lag) if d == 1)
        own = sum(1 for x in range(g) for d, _ in after(x, lag) if d == 0)
        behind = sum(1 for x in range(g, NG) for d, _ in after(x, lag) if d == -1)
        early = sum(1 for x in range(NG) for d, _ in after(x, lag) if d == 1)
        number = t * QB - behind + own + early + ahead
        return min(number, units * QB) if isinstance(number, int) else number

    parts_v = parts1.rearrange("a r b (g h d) n -> (b g) a r d h n", g=H1 // G1, h=G1)
    o1_v = o1.rearrange("(b q s p) (g e) -> b g q p s e", b=B, p=P, s=S, g=H1 // G1)

    with ExitStack() as ctx:
        sb, pb, sem = names(nc, ctx, "attend1")
        qs, ks = sb("qs", [R + 1, 2, G1, T], BF16), sb("ks", [R + 1, 2, G1, T], BF16)
        v = sb("v", [P, 2, KT, G1 * HV])
        probs = sb("probs", [P, RING, BLOCK])
        part = sb("part", [P, G1, S, 1 + QB - 1])
        masked_out = sb("masked_out", [P, 2, BLOCK])
        peak, row = sb("peak", [P, G1 * S]), sb("row", [G1 * S, 2, P], BF16)
        u, inv = sb("u", [P, BLOCK]), sb("inv", [P, S, G1])
        out = sb("out", [P, 2, S, G1, DH1])
        score_ps, chunk_ps = pb("score_ps", [P, BANKS, BLOCK]), pb("chunk_ps", [P, CBANKS, BLOCK])
        pv_ps, turn_ps = (pb(n, [P, BLOCK]) for n in ("pv_ps", "turn_ps"))

        consts, unit_in = sem("consts"), sem("unit_in", 2)
        chunk_ready, chunk_read = sem("chunk_ready"), sem("chunk_read")
        peaked, peak_turned, row_ready, row_in = sem("peaked"), sem("peak_turned"), sem("row_ready"), sem("row_in", 2)
        scores_ready, exp_done, masked, pv_done = sem("scores_ready"), sem("exp_done"), sem("masked"), sem("pv_done")
        u_ready, u_turned, inverted, out_ready, out_stored = (sem("u_ready"), sem("u_turned"), sem("inverted"),
                                                              sem("out_ready"), sem("out_stored", 2))
        LOADS = 2 * 6 + 1
        block = ctx.enter_context(nc.Block())

        @block.sync
        def _(e):
            def load(s):
                wait(e, pv_done, (s.t - 1) * NG)
                for r, (tile, order) in enumerate(((qs, Q_PARTS), (ks, K_PARTS))):
                    for n, a in enumerate(order):
                        e.dma_start(tile[n * DH1:(n + 1) * DH1, s.slot], at_step(parts_v, s.t)[a, r]).then_inc(unit_in[s.slot], 16)
                e.dma_start(v[:, s.slot], at_step(v1, s.t)).then_inc(unit_in[s.slot], 16)

            def body(at):
                if at(1) is not None:
                    load(at(1))
                for g in range(NG):
                    for d, q in after_maxima(g, 3):
                        s = at(d)
                        if s is not None:
                            e.wait_ge(row_ready, s.t * QB + q + 1)
                            for h in range(G1):
                                e.dma_start(qs[R:R + 1, s.slot, h, q * BLOCK:(q + 1) * BLOCK].rearrange("o (s p) -> o s p", s=S),
                                            row[h * S:(h + 1) * S, q % 2]).then_inc(row_in[q % 2], 16)
                    for d, q in after_block(g, 4):
                        s = at(d)
                        if s is not None:
                            e.wait_ge(out_ready, s.t * QB + q + 1)
                            hold(e, passed)
                            e.dma_start(at_step(at_step(o1_v, s.t // (H1 // G1)), s.t % (H1 // G1))[q],
                                        out[:, q % 2].rearrange("p s h d -> p s (h d)")).then_inc(out_stored[q % 2], 16)

            pipelined(e, units, 2, body)
            for n in range(2):
                e.wait_ge(out_stored[n], 16 * units * QB // 2)

        @block.tensor
        def _(e):
            e.wait_ge(consts, 1)

            def chunk(s, n):
                q, j, h, kc = CHUNKS[n]
                if n == 0:
                    e.wait_ge(unit_in[s.slot], (s.turn + 1) * 16 * LOADS)
                wait(e, chunk_read, s.t * N + chunk_before[n] + 1)
                width = BLOCK if kc < q else (j + 1) * P
                tile = q * BLOCK + j * P
                e.matmul(chunk_ps[:, n % CBANKS, 0:width], qs[0:R, s.slot, h, tile:tile + P],
                         ks[0:R, s.slot, h, kc * BLOCK:kc * BLOCK + width], start=True, stop=True).then_inc(chunk_ready, 1)

            def pv(s, g):
                q, kt = GROUPS[g]
                if kt == 0:
                    wait(e, u_ready, s.t * QB + q)
                e.wait_ge(exp_done, s.t * N + (g + 1) * G1)
                if kt >= S * q:
                    e.wait_ge(masked, s.t * MASKED[-1] + MASKED[g])
                off = max(0, kt - S * q) * P
                for h in range(G1):
                    mm = e.matmul(pv_ps[h * HV:(h + 1) * HV, off:], v[:, s.slot, kt, h * HV:(h + 1) * HV],
                                  probs[:, (g * G1 + h) % RING, off:], start=(kt == 0), stop=(g == LAST[q]))
                mm.then_inc(pv_done, 1)

            def body(at):
                cur = at(0)
                for g in range(NG):
                    q, kt = GROUPS[g]
                    off = max(0, kt - S * q) * P
                    for what, h in (("score", 0), ("chunk", 0), ("score", 1), ("chunk", 1), ("score", 2), ("chunk", 2),
                                    ("score", 3), ("turn", 0), ("pv", 0), ("chunk", 3)):
                        x = g * G1 + h
                        if what == "score" and cur is not None:
                            if kt == 0 and h == 0:
                                e.wait_ge(row_in[q % 2], (cur.t * 2 + q // 2 + 1) * 16 * G1)
                            wait(e, exp_done, cur.t * N + before[x] + 1)
                            e.matmul(score_ps[:, x % BANKS, off:], ks[:, cur.slot, h, kt * P:(kt + 1) * P],
                                     qs[:, cur.slot, h, q * BLOCK + off:(q + 1) * BLOCK], start=True, stop=True)\
                                .then_inc(scores_ready, 1)
                        if what == "chunk":
                            d, n = chunk_at(x)
                            if at(d) is not None and (d == 1 or cur is not None):
                                chunk(at(d), n)
                        if what == "turn":
                            for d, q_ in after_maxima(g, 2):
                                s = at(d)
                                if s is not None:
                                    e.wait_ge(peaked, s.t * QB + q_ + 1)
                                    wait(e, row_ready, s.t * QB + q_)
                                    wait(e, out_ready, turns_before(at, g, after_block, 3))
                                    e.transpose(turn_ps[0:G1 * S, 0:P], peak[:], ident).then_inc(peak_turned, 1)
                        if what == "pv" and g == 0 and at(-1) is not None:
                            pv(at(-1), NG - 1)
                        if what == "pv" and g > 0 and cur is not None:
                            pv(cur, g - 1)
                    for d, q_ in after_block(g, 3):
                        s = at(d)
                        if s is not None:
                            e.wait_ge(u_ready, s.t * QB + q_ + 1)
                            wait(e, out_ready, s.t * QB + q_)
                            wait(e, row_ready, turns_before(at, g + 1, after_maxima, 2))
                            for j in range(S):
                                mm = e.transpose(turn_ps[:, j * P:(j + 1) * P], u[:, j * P:(j + 1) * P], ident)
                            mm.then_inc(u_turned, 1)

            pipelined(e, units, 2, body)

        @block.scalar
        def _(e):
            def body(at):
                for g in range(NG):
                    q, kt = GROUPS[g]
                    off = max(0, kt - S * q) * P
                    if at(0) is not None:
                        s = at(0)
                        wait(e, pv_done, s.t * NG + g - RING // G1 + 1)
                        for h in range(G1):
                            x = g * G1 + h
                            e.wait_ge(scores_ready, s.t * N + x + 1)
                            e.activation(probs[:, x % RING, off:], score_ps[:, x % BANKS, off:], ACT.Exp,
                                         scale=DH1 ** -0.5).then_inc(exp_done, 1)
                    for d, q_ in after_block(g, 1):
                        s = at(d)
                        if s is not None:
                            e.wait_ge(pv_done, s.t * NG + LAST[q_] + 1)
                            wait(e, u_turned, s.t * QB + q_)
                            e.activation(u[:], pv_ps[:], ACT.Copy).then_inc(u_ready, 1)

            pipelined(e, units, 2, body)

        @block.gpsimd
        def _(e):
            def body(at):
                s = at(0)
                if s is None:
                    return
                for g in range(NG):
                    q, kt = GROUPS[g]
                    if kt < S * q:
                        continue
                    off = (kt - S * q) * P
                    for h in range(G1):
                        x = g * G1 + h
                        e.wait_ge(exp_done, s.t * N + x + 1)
                        hold(e, passed)
                        tile = probs[:, x % RING, off:off + P]
                        e.affine_select(out=tile, in_=tile, compare_op=ALU.is_ge, fill=0.0, base=0,
                                        pattern=[[1, P]], channel_multiplier=-1).then_inc(masked, 1)

            pipelined(e, units, 2, body)

        @block.vector
        def _(e):
            e.memset(ks[R:R + 1], 1.0).then_inc(consts, 1)

            def read(s, n):
                q, j, h, kc = CHUNKS[n]
                if j == 0 and h == 0 and kc == 0:
                    wait(e, peaked, s.t * QB + q)
                src = chunk_ps[:, n % CBANKS]
                e.wait_ge(chunk_ready, s.t * N + n + 1)
                if kc < q:
                    e.tensor_reduce(part[:, h, j, 1 + kc:2 + kc], src, AX.X, ALU.max).then_inc(chunk_read, 1)
                    return
                wait(e, chunk_read, s.t * N + n - 1)
                hold(e, passed)
                width = (j + 1) * P
                e.tensor_tensor_reduce(masked_out[:, n % 2, 0:width], src[:, 0:width], upper[:, BLOCK - width:], 1.0, LOWEST,
                                       ALU.add, ALU.max, part[:, h, j, 0:1]).then_inc(chunk_read, 1)

            def body(at):
                cur = at(0)
                for g in range(NG):
                    for d, q in after_maxima(g, 3):
                        s = at(d)
                        if s is not None:
                            e.wait_ge(peak_turned, s.t * QB + q + 1)
                            wait(e, row_in[q % 2], (s.t * 2 + q // 2) * 16 * G1)
                            e.tensor_copy(row[:, q % 2], turn_ps[0:G1 * S, 0:P]).then_inc(row_ready, 1)
                    for d, q in after_block(g, 4):
                        s = at(d)
                        if s is not None:
                            e.wait_ge(u_turned, s.t * QB + q + 1)
                            t_ = turn_ps[:].rearrange("p (s h e) -> p s h e", s=S, h=G1)
                            wait(e, out_ready, s.t * QB + q)
                            e.reciprocal(inv[:], t_[:, :, :, DH1]).then_inc(inverted, 1)
                            e.wait_ge(inverted, s.t * QB + q + 1)
                            wait(e, out_stored[q % 2], (s.t * 2 + q // 2) * 16)
                            e.tensor_tensor(out[:, q % 2], t_[:, :, :, 0:DH1],
                                            inv[:].unsqueeze(3).broadcast_to([P, S, G1, DH1]), ALU.mult).then_inc(out_ready, 1)
                    for h in range(G1):
                        d, n = chunk_at(g * G1 + h)
                        if at(d) is not None and (d == 1 or cur is not None):
                            read(at(d), n)
                    for d, q in after_maxima(g, 0):
                        s = at(d)
                        if s is not None:
                            e.wait_ge(chunk_read, s.t * N + CHUNK_END[q])
                            wait(e, peak_turned, s.t * QB + q)
                            e.tensor_reduce(peak[:], part[:, :, :, 0:1 + q].rearrange("p h s n -> p (h s) n"), AX.X, ALU.max,
                                            negate=True).then_inc(peaked, 1)

            pipelined(e, units, 2, body)


def close(nc, o1, base, W_o, out, ident):
    o1_v = o1.rearrange("(t s p) e -> t p s e", p=P, s=S)
    base_v = base.rearrange("(t s p) d -> t p s d", p=P, s=S)
    out_v = out.rearrange("b (q s p) d -> (b q) p s d", p=P, s=S)
    with ExitStack() as ctx:
        sb, pb, sem = names(nc, ctx, "close")
        wo = sb("wo", [P, C, D])
        oin, bin_ = sb("oin", [P, 4, S, D]), sb("bin", [P, 4, S, D])
        ot, total = sb("ot", [P, 2, C, BLOCK]), sb("total", [P, 2, S, D])
        turn_ps, y_ps = pb("turn_ps", [P, 2, C, BLOCK]), pb("y_ps", [P, 2, S, D])
        weights_in, block_in = sem("weights_in"), sem("block_in", 4)
        turned, ot_ready, projected, total_ready, stored = (sem("turned"), sem("ot_ready"), sem("projected"),
                                                            sem("total_ready"), sem("stored", 2))
        block = ctx.enter_context(nc.Block())

        @block.sync
        def _(e):
            e.dma_start(wo[:], W_o.rearrange("(c p) h -> p c h", p=P)).then_inc(weights_in, 16)

            def body(at):
                nxt, cur = at(3), at(0)
                if nxt is not None:
                    s = nxt
                    wait(e, turned, s.t - 3)
                    e.dma_start(oin[:, s.place], at_step(o1_v, s.t)).then_inc(block_in[s.place], 16)
                    wait(e, total_ready, s.t - 3)
                    e.dma_start(bin_[:, s.place], at_step(base_v, s.t)).then_inc(block_in[s.place], 16)
                if cur is not None:
                    s = cur
                    e.wait_ge(total_ready, s.t + 1)
                    e.dma_start(at_step(out_v, s.t), total[:, s.slot]).then_inc(stored[s.slot], 16)

            pipelined(e, NBLK, 4, body, ahead=3)
            for slot in range(2):
                e.wait_ge(stored[slot], 16 * NBLK // 2)

        @block.tensor
        def _(e):
            e.wait_ge(weights_in, 16)

            def body(at):
                nxt, cur = at(1), at(0)
                if nxt is not None:
                    s = nxt
                    e.wait_ge(block_in[s.place], (s.stay + 1) * 32)
                    wait(e, ot_ready, s.t - 1)
                    for j in range(S):
                        for c in range(C):
                            mm = e.transpose(turn_ps[:, s.slot, c, j * P:(j + 1) * P], oin[:, s.place, j, c * P:(c + 1) * P], ident)
                    mm.then_inc(turned, 1)
                if cur is not None:
                    s = cur
                    e.wait_ge(ot_ready, s.t + 1)
                    wait(e, total_ready, s.t - 1)
                    for j in range(S):
                        for c in range(C):
                            mm = e.matmul(y_ps[:, s.slot, j], ot[:, s.slot, c, j * P:(j + 1) * P], wo[:, c],
                                          start=(c == 0), stop=(c == C - 1))
                    mm.then_inc(projected, 1)

            pipelined(e, NBLK, 4, body)

        @block.scalar
        def _(e):
            def body(at):
                s = at(0)
                if s is None:
                    return
                e.wait_ge(turned, s.t + 1)
                wait(e, projected, s.t - 1)
                e.activation(ot[:, s.slot], turn_ps[:, s.slot], ACT.Copy).then_inc(ot_ready, 1)

            pipelined(e, NBLK, 4, body)

        @block.vector
        def _(e):
            def body(at):
                s = at(0)
                if s is None:
                    return
                e.wait_ge(projected, s.t + 1)
                e.wait_ge(block_in[s.place], (s.stay + 1) * 32)
                wait(e, stored[s.slot], s.turn * 16)
                e.tensor_tensor(total[:, s.slot], y_ps[:, s.slot], bin_[:, s.place], ALU.add).then_inc(total_ready, 1)

            pipelined(e, NBLK, 4, body)


_INS = {
    "L0_attn_x": "x", "L0_attn_Wa": "Wa", "L0_attn_Wx": "Wx", "L0_attn_ba": "ba", "L0_attn_bx": "bx", "L0_attn_Lam": "Lam",
    "L0_ffn_Wq": "Wq0", "L0_ffn_bq": "bq0", "L0_ffn_Wk": "Wk0", "L0_ffn_bk": "bk0", "L0_ffn_Wv": "Wv0", "L0_ffn_bv": "bv0",
    "L0_ffn_Wr": "Wr0", "L0_ffn_br": "br0", "L0_ffn_Wo": "Wo0", "L0_ffn_bo": "bo0",
    "L1_attn_W_q": "Wq1", "L1_attn_b_q": "bq1", "L1_attn_W_k": "Wk1", "L1_attn_b_k": "bk1",
    "L1_attn_W_v": "Wv1", "L1_attn_b_v": "bv1", "L1_attn_W_o": "Wo1", "L1_attn_b_o": "bo1",
    "L1_ffn_W_r": "W_r", "L1_ffn_W_k": "W_k", "L1_ffn_W_v": "W_v", "L1_ffn_mu_r": "mu_r", "L1_ffn_mu_k": "mu_k",
}


def program(nc, out, x, Wa, Wx, ba, bx, Lam, Wq0, bq0, Wk0, bk0, Wv0, bv0, Wr0, br0, Wo0, bo0,
            Wq1, bq1, Wk1, bk1, Wv1, bv1, Wo1, bo1, W_r, W_k, W_v, mu_r, mu_k):
    def dram(name, shape, dt=F32):
        return nc.dram_tensor(name, shape, dt, kind="Internal").ap()

    nc.disable_value_cache = True
    yT = dram("yT", (D, B * T))
    chosen, gates = dram("chosen", (B * K0,), U32), dram("gates", (B * K0,))
    qk_hi, qk_lo = dram("qk_hi", (2, B * K0, DH0, T)), dram("qk_lo", (2, B * K0, DH0, T))
    v0, o0 = dram("v0", (B, P, KT, K0 * DH0)), dram("o0", (B * T, K0 * DH0))
    parts1, v1 = dram("parts1", (3, 2, B, D, T), BF16), dram("v1", (B * H1 // G1, P, KT, G1 * 2 * DH1))
    base, o1 = dram("base", (B * T, D)), dram("o1", (B * T, D))
    with ExitStack() as ctx:
        sb, _, sem = names(nc, ctx, "program")
        passed = sem("passed")
        ident, fold, upper = sb("ident", [P, P]), sb("fold", [P, DH0]), sb("upper", [P, BLOCK])
        means = sb("means", [P, C, B])
        constants(nc, ident[:], fold[:], upper[:])
        with nc.sbuf_tensor("program_xnT", [P, C, B * T], F32) as xnT:
            recurrence(nc, x, Wa, Wx, ba, bx, Lam, xnT, yT, means, ident[:], passed)
            route(nc, means, Wr0, br0, chosen, gates)
            project0(nc, xnT, Wq0, Wk0, Wv0, bq0, bk0, bv0, chosen, qk_hi, qk_lo, v0, passed)
        attend0(nc, qk_hi, qk_lo, v0, gates, o0, ident[:], fold[:], passed)
        between(nc, x, o0, yT, Wo0, bo0, Wq1, Wk1, Wv1, bq1, bk1, bv1, bo1, W_r, W_k, W_v, mu_r, mu_k,
                ident[:], parts1, v1, base, passed)
        attend1(nc, parts1, v1, o1, ident[:], upper[:], passed)
        close(nc, o1, base, Wo1, out, ident[:])


def kernel(**inputs):
    import concourse.bacc as bacc
    from concourse.bass_utils import run_bass_kernel_spmd

    nc = bacc.Bacc("TRN2", target_bir_lowering=False, num_devices=1)
    arrays, args = {}, {}
    for name, short in _INS.items():
        a = np.ascontiguousarray(inputs[name])
        arrays[f"in_{name}"] = a
        args[short] = nc.dram_tensor(f"in_{name}", a.shape, mybir.dt.from_np(a.dtype), kind="ExternalInput").ap()
    out = nc.dram_tensor("out", (B, T, D), F32, kind="ExternalOutput").ap()
    program(nc, out, **args)
    return run_bass_kernel_spmd(nc, [arrays], core_ids=[0]).results[0]["out"]
```
